# Optimizing a Trainium2 kernel written in Bass

```python
import numpy as np
import jax
import jax.numpy as jnp

def _softmax(x, axis=-1):
    return jax.nn.softmax(x, axis=axis)

def _gelu(x):
    return jax.nn.gelu(x, approximate=True)

def _silu(x):
    return jax.nn.silu(x)

def _sigmoid(x):
    return jax.nn.sigmoid(x)

def _layernorm(x, axis=-1, eps=1e-05):
    m = jnp.mean(x, axis=axis, keepdims=True)
    v = jnp.var(x, axis=axis, keepdims=True)
    return (x - m) / jnp.sqrt(v + eps)

def _scatter_add(tgt, idx, src, axis=0):
    return tgt.at[idx].add(src)

def _segment_sum(src, seg, n):
    return jax.ops.segment_sum(src, seg, n)
kernel_name = 'mk_prb_d1_jaxref_r8_c0c512'

def setup_inputs(seed: int=0):
    np.random.seed(seed)
    _w = jnp.asarray

    def _L0_attn_setup():
        import jax, jax.numpy as jnp
        import numpy as np
        BATCH, SEQ, HIDDEN = (2, 512, 512)
        HEADS, HEAD_DIM, BLOCK = (32, 128, 32)
        LAYER_IDX, N_LAYERS = (1, 32)
        EPS = 1e-05

        def _decays():
            base = 1.0 / 2.0 ** (8.0 / HEADS)
            exponent = jnp.arange(HEADS, dtype=jnp.float32) + 1.0
            factor = 1.0 - LAYER_IDX / (N_LAYERS - 1 + 1e-05) + 1e-05
            slope = (base ** exponent * factor)[:, None, None]
            r = jnp.arange(BLOCK, dtype=jnp.float32) + 1.0
            q_decay = jnp.exp(-slope * r[:, None])
            k_decay = jnp.exp(-slope * (BLOCK - r)[:, None])
            diff = r[:, None] - r[None, :]
            diag = slope[None] * diff[None, None]
            diag = jnp.where(diag >= 0, -diag, -jnp.inf)
            diag_decay = jnp.exp(diag)
            block_decay = jnp.exp(-slope * BLOCK)
            return (q_decay, k_decay, diag_decay, block_decay)
        key = jax.random.key(seed)
        ks = jax.random.split(key, 5)
        s = 0.02
        return {'hidden_states': jax.random.normal(ks[0], (BATCH, SEQ, HIDDEN), jnp.float32), 'qkv_w': jax.random.normal(ks[1], (3 * HEADS * HEAD_DIM, HIDDEN), jnp.float32) * s, 'out_w': jax.random.normal(ks[2], (HIDDEN, HEADS * HEAD_DIM), jnp.float32) * s, 'gate_w': jax.random.normal(ks[3], (HEADS * HEAD_DIM, HIDDEN), jnp.float32) * s, 'norm_w': jnp.ones((HEADS * HEAD_DIM,), jnp.float32)}
    _L0_attn_in = _L0_attn_setup()

    def _L0_ffn_setup():
        import jax, jax.numpy as jnp
        import numpy as np
        R = 16
        NUM_EXPERTS = 8
        TOP_K = 2
        LORA_ALPHA = 32
        SCALING = LORA_ALPHA / R
        key = jax.random.key(seed)
        ks = jax.random.split(key, 6)
        d_in, d_out = (512, 512)
        x = jax.random.normal(ks[0], (4, 256, d_in), dtype=jnp.float32)
        W_base = jax.random.normal(ks[1], (d_out, d_in), dtype=jnp.float32) * 0.02
        b_base = jax.random.normal(ks[2], (d_out,), dtype=jnp.float32) * 0.02
        W_router = jax.random.normal(ks[3], (NUM_EXPERTS, d_in), dtype=jnp.float32) * 0.01
        A = jax.random.normal(ks[4], (NUM_EXPERTS, R, d_in), dtype=jnp.float32) * 0.02
        B = jax.random.normal(ks[5], (NUM_EXPERTS, d_out, R), dtype=jnp.float32) * 0.02
        return {'x': x, 'W_base': W_base, 'b_base': b_base, 'W_router': W_router, 'A': A, 'B': B}
    _L0_ffn_in = _L0_ffn_setup()
    _d = {'L0_attn_hidden_states': _L0_attn_in['hidden_states'], 'L0_attn_qkv_w': _L0_attn_in['qkv_w'], 'L0_attn_out_w': _L0_attn_in['out_w'], 'L0_attn_gate_w': _L0_attn_in['gate_w'], 'L0_attn_norm_w': _L0_attn_in['norm_w'], 'L0_ffn_W_base': _L0_ffn_in['W_base'], 'L0_ffn_b_base': _L0_ffn_in['b_base'], 'L0_ffn_W_router': _L0_ffn_in['W_router'], 'L0_ffn_A': _L0_ffn_in['A'], 'L0_ffn_B': _L0_ffn_in['B']}
    _x0 = _d['L0_attn_hidden_states']
    _d['L0_attn_hidden_states'] = jax.random.normal(jax.random.fold_in(jax.random.key(seed), 1), (2, 512, 512), dtype=_x0.dtype)
    del _x0
    return _d

def reference(L0_attn_hidden_states, L0_attn_qkv_w, L0_attn_out_w, L0_attn_gate_w, L0_attn_norm_w, L0_ffn_W_base, L0_ffn_b_base, L0_ffn_W_router, L0_ffn_A, L0_ffn_B):

    def _L0_attn_ref(hidden_states, qkv_w, out_w, gate_w, norm_w):
        import jax, jax.numpy as jnp
        import numpy as np
        BATCH, SEQ, HIDDEN = (2, 512, 512)
        HEADS, HEAD_DIM, BLOCK = (32, 128, 32)
        LAYER_IDX, N_LAYERS = (1, 32)
        EPS = 1e-05

        def _decays():
            base = 1.0 / 2.0 ** (8.0 / HEADS)
            exponent = jnp.arange(HEADS, dtype=jnp.float32) + 1.0
            factor = 1.0 - LAYER_IDX / (N_LAYERS - 1 + 1e-05) + 1e-05
            slope = (base ** exponent * factor)[:, None, None]
            r = jnp.arange(BLOCK, dtype=jnp.float32) + 1.0
            q_decay = jnp.exp(-slope * r[:, None])
            k_decay = jnp.exp(-slope * (BLOCK - r)[:, None])
            diff = r[:, None] - r[None, :]
            diag = slope[None] * diff[None, None]
            diag = jnp.where(diag >= 0, -diag, -jnp.inf)
            diag_decay = jnp.exp(diag)
            block_decay = jnp.exp(-slope * BLOCK)
            return (q_decay, k_decay, diag_decay, block_decay)
        b, s, _ = hidden_states.shape
        h, d, bs = (HEADS, HEAD_DIM, BLOCK)
        nb = s // bs
        q_decay, k_decay, diag_decay, block_decay = _decays()
        qkv = jax.nn.silu(hidden_states @ qkv_w.T)
        qkv = qkv.reshape(b, s, h, 3, d)
        q = jnp.moveaxis(qkv[:, :, :, 0], 2, 1)
        k = jnp.moveaxis(qkv[:, :, :, 1], 2, 1)
        v = jnp.moveaxis(qkv[:, :, :, 2], 2, 1)

        def to_blocks(x):
            return jnp.moveaxis(x.reshape(b, h, nb, bs, d), 2, 0)
        qb, kb, vb = (to_blocks(q), to_blocks(k), to_blocks(v))

        def step(kv, blk):
            cq, ck, cv = blk
            scores = jnp.einsum('bhnd,bhmd->bhnm', cq, ck) * diag_decay
            intra = jnp.einsum('bhnm,bhmd->bhnd', scores, cv)
            inter = jnp.einsum('bhnd,bhde->bhne', cq * q_decay, kv)
            kv_next = kv * block_decay + jnp.einsum('bhnd,bhne->bhde', ck * k_decay, cv)
            return (kv_next, intra + inter)
        kv0 = jnp.zeros((b, h, d, d), hidden_states.dtype)
        _, out_blocks = jax.lax.scan(step, kv0, (qb, kb, vb))
        attn = jnp.moveaxis(out_blocks, 0, 2)
        attn = attn.reshape(b, h, s, d).transpose(0, 2, 1, 3).reshape(b, s, h * d)
        xf = attn.astype(jnp.float32)
        xf = xf * jax.lax.rsqrt(jnp.mean(xf * xf, axis=-1, keepdims=True) + EPS)
        normed = norm_w * xf.astype(attn.dtype)
        gate = jax.nn.sigmoid(hidden_states @ gate_w.T)
        return gate * normed @ out_w.T

    def _L0_ffn_ref(x, W_base, b_base, W_router, A, B):
        import jax, jax.numpy as jnp
        import numpy as np
        R = 16
        NUM_EXPERTS = 8
        TOP_K = 2
        LORA_ALPHA = 32
        SCALING = LORA_ALPHA / R
        orig_shape = x.shape
        d_in = x.shape[-1]
        x_flat = x.reshape(-1, d_in)
        logits = x_flat @ W_router.T
        probs = jax.nn.softmax(logits, axis=-1)
        topk_probs, topk_idx = jax.lax.top_k(probs, TOP_K)
        topk_probs = topk_probs / jnp.sum(topk_probs, axis=-1, keepdims=True)
        onehot = jax.nn.one_hot(topk_idx, NUM_EXPERTS, dtype=x.dtype)
        combine = jnp.einsum('nk,nke->ne', topk_probs, onehot)
        h = jnp.einsum('nd,erd->ner', x_flat, A)
        hw = h * combine[:, :, None]
        expert_out = jnp.einsum('ner,eor->no', hw, B) * SCALING
        base_out = x_flat @ W_base.T + b_base
        out = base_out + expert_out
        return out.reshape(*orig_shape[:-1], W_base.shape[0])
    x = L0_attn_hidden_states
    xn = _layernorm(x, axis=-1)
    x = x + _L0_attn_ref(xn, L0_attn_qkv_w, L0_attn_out_w, L0_attn_gate_w, L0_attn_norm_w) + _L0_ffn_ref(xn, L0_ffn_W_base, L0_ffn_b_base, L0_ffn_W_router, L0_ffn_A, L0_ffn_B)
    return x

_drawn_inputs = setup_inputs


def setup_inputs(seed=0):
    import zlib

    import numpy as np

    out = dict(_drawn_inputs(seed))
    spreads = {'L0_attn_norm_w': (1.0, 0.2)}
    factors = {'L0_ffn_b_base': 3.786}
    for name, (base, spread) in spreads.items():
        noise = np.random.default_rng([zlib.crc32(name.encode()), seed]).standard_normal(out[name].shape)
        drawn = base * np.exp(spread * noise) if base else spread * noise
        out[name] = jnp.asarray(drawn.astype(out[name].dtype))
    for name, factor in factors.items():
        out[name] = (out[name] * factor).astype(out[name].dtype)
    return out
```

```python
from contextlib import ExitStack

import concourse.bass as bass
from concourse import mybir

F32 = mybir.dt.float32
F32R = mybir.dt.float32r
ALU = mybir.AluOpType
ACT = mybir.ActivationFunctionType
AX = mybir.AxisListType

P = 128
BATCH, SEQ, HID = 2, 512, 512
HEADS, D = 32, 128
KC = HID // P
TB = SEQ // P
NTB = BATCH * TB
GH = 2
GROUPS = HEADS // GH
STEPS = GH * BATCH
EXPERTS, RANK, TOP_K = 8, 16, 2
ER = EXPERTS * RANK
LORA_SCALING = 32 / RANK
EPS = 1e-5
V_AT = (1, 1 + TB)
PROJ = 3 * STEPS + NTB
PROJ0 = (0, 3 + TB, 2 * (3 + TB), 2 * (3 + TB) + 3)
S_FROM = tuple(min(P * j, SEQ - 256) for j in range(TB))
S_LEN = tuple(SEQ - f for f in S_FROM)
P_AT = tuple(sum(S_LEN[:j]) for j in range(TB))
P_COLS = sum(S_LEN)
F_LEN = tuple(SEQ - P * j for j in range(TB))
F_AT = tuple(sum(F_LEN[:j]) for j in range(TB))
FIRST_CHUNKS = 5
RAW_SLOTS = 5
GROUP_CHUNKS = 10


def at_least(eng, sem, value):
    if isinstance(value, int) and value <= 0:
        return
    eng.wait_ge(sem, value)


def build(nc, x, w_chunks, norm_w, a_router, b_base, slopes, out):
    x_tok = x.rearrange("b (t p) c -> p (b t) c", p=P)
    out_tok = out.rearrange("b (t p) c -> p (b t) c", p=P)

    ctx = ExitStack()
    with ctx:
        def sb(name, shape, dt=F32):
            return ctx.enter_context(nc.sbuf_tensor(name, shape, dt))

        def bank(name):
            return ctx.enter_context(nc.psum_tensor(name, [P, 512], F32))

        def sem(name):
            return ctx.enter_context(nc.semaphore(name))

        xhi = sb("xhi", [P, KC, BATCH * SEQ], F32R)
        xlo = sb("xlo", [P, KC, BATCH * SEQ], F32R)
        acc = sb("acc", [P, NTB, HID])
        decay = sb("decay", [P, HEADS, 2 * P])
        table = sb("table", [P, SEQ])
        raw = sb("raw", [P, RAW_SLOTS, 512])
        qkg_hi = [sb(f"qkg_hi{i}", [P, 3, KC * P], F32R) for i in range(GH)]
        qkg_lo = [sb(f"qkg_lo{i}", [P, 3, KC * P], F32R) for i in range(GH)]
        wv_hi = sb("wv_hi", [P, 2, 512], F32R)
        wv_lo = sb("wv_lo", [P, 2, 512], F32R)
        wo_hi = sb("wo_hi", [P, GH, HID], F32R)
        wo_lo = sb("wo_lo", [P, GH, HID], F32R)
        qf = sb("qf", [P, SEQ])
        kf = sb("kf", [P, SEQ])
        q_hi = sb("q_hi", [P, SEQ], F32R)
        q_lo = sb("q_lo", [P, SEQ], F32R)
        k_hi = sb("k_hi", [P, SEQ], F32R)
        k_lo = sb("k_lo", [P, SEQ], F32R)
        vf = [sb(f"vf{i}", [P, GH * D]) for i in range(TB)]
        v_hi = [sb(f"v_hi{b}", [P, TB, GH * D], F32R) for b in range(BATCH)]
        v_lo = [sb(f"v_lo{b}", [P, TB, GH * D], F32R) for b in range(BATCH)]
        pf = sb("pf", [P, sum(F_LEN)])
        p_hi = sb("p_hi", [P, P_COLS], F32R)
        p_lo = sb("p_lo", [P, P_COLS], F32R)
        tanh_g = sb("tanh_g", [P, SEQ])
        square = sb("square", [P, SEQ])
        gated = sb("gated", [P, SEQ])
        g_hi = [sb(f"g_hi{s}", [P, SEQ], F32R) for s in range(STEPS)]
        g_lo = [sb(f"g_lo{s}", [P, SEQ], F32R) for s in range(STEPS)]
        sum_sq = sb("sum_sq", [P, BATCH, SEQ])
        ident = sb("ident", [P, P])
        ones = sb("ones", [P, 1])
        slope = sb("slope", [P, HEADS])
        far = sb("far", [P, 2, HEADS])
        norm = sb("norm", [P, HEADS])
        half_norm = sb("half_norm", [P, HEADS])
        minus_half = sb("minus_half", [P, NTB])
        stats = sb("stats", [P, NTB, 6])
        mean_var = sb("mean_var", [P, NTB, 2])
        rs = sb("rs", [P, 4, NTB])

        diff = square[:, 0:2 * P]
        free = decay[:, :, :].rearrange("p h n -> p (h n)")
        taken = [0]

        def take(*shape):
            n = 1
            for d in shape:
                n *= d
            part = free[:, taken[0]:taken[0] + n]
            taken[0] += n
            if len(shape) == 1:
                return part
            names = "abc"[:len(shape)]
            sizes = {k: d for k, d in zip(names, shape)}
            return part.rearrange(f"p ({' '.join(names)}) -> p {' '.join(names)}", **sizes)

        x_again = take(NTB, HID)
        ar = take(KC, ER + EXPERTS)
        base_b = take(HID)
        h_keep = take(NTB, ER)
        sm = [take(NTB, EXPERTS) for _ in range(8)]
        sm1 = [take(NTB) for _ in range(8)]
        xf = [qf, kf]
        hw_hi = g_hi[0:2]
        hw_lo = g_lo[0:2]

        proj = [bank(f"proj{i}") for i in range(2)]
        score = [bank(f"score{i}") for i in range(3)]
        att = bank("att")
        outp = [bank(f"outp{i}") for i in range(2)]
        S = [score[j % 3][:, 0:S_LEN[j]] for j in range(TB)]

        x_in = [sem(f"x_in{b}") for b in range(BATCH)]
        slope_in = sem("slope_in")
        raw_in = [sem(f"raw_in{i}") for i in range(RAW_SLOTS)]
        norm_in = sem("norm_in")
        again_in = sem("again_in")
        consts = sem("consts")
        diff_made = sem("diff_made")
        decay_made = sem("decay_made")
        ln = sem("ln")
        pow_ready = sem("pow_ready")
        pow_done = sem("pow_done")
        xn_ready = sem("xn_ready")
        turned = sem("turned")
        xhi_done = sem("xhi_done")
        xlo_done = sem("xlo_done")
        acc_zero = sem("acc_zero")
        whi_done = sem("whi_done")
        wlo_done = sem("wlo_done")
        proj_ready = sem("proj_ready")
        proj_free = sem("proj_free")
        qhi_done = sem("qhi_done")
        qlo_done = sem("qlo_done")
        khi_done = sem("khi_done")
        klo_done = sem("klo_done")
        vhi_done = sem("vhi_done")
        vlo_done = sem("vlo_done")
        gate_done = sem("gate_done")
        table_done = sem("table_done")
        scores_ready = sem("scores_ready")
        masked = sem("masked")
        phi_done = sem("phi_done")
        plo_done = sem("plo_done")
        att_ready = sem("att_ready")
        gated_done = sem("gated_done")
        ghi_done = sem("ghi_done")
        glo_done = sem("glo_done")
        square_done = sem("square_done")
        summed = sem("summed")
        out_ready = sem("out_ready")
        acc_done = sem("acc_done")
        late_in = sem("late_in")
        xf_done = sem("xf_done")
        h_ready = sem("h_ready")
        h_read = sem("h_read")
        route = sem("route")
        route_act = sem("route_act")
        rms_ready = sem("rms_ready")
        hw_done = sem("hw_done")
        hw_turned = sem("hw_turned")
        hwhi_done = sem("hwhi_done")
        hwlo_done = sem("hwlo_done")
        xb_done = sem("xb_done")
        part_done = sem("part_done")
        ffn_ready = sem("ffn_ready")
        result_done = sem("result_done")
        stored = sem("stored")

        def chunk(kind, i, c):
            hi, lo = {"qkg": (qkg_hi[i], qkg_lo[i]), "v": (wv_hi, wv_lo), "o": (wo_hi, wo_lo)}[kind]
            return hi[:, c, :], lo[:, c, :]

        def first_weights():
            return [chunk("qkg", 0, 0), chunk("qkg", 0, 1), chunk("qkg", 0, 2), chunk("v", 0, 0), chunk("v", 0, 1)]

        def weights():
            return [chunk("qkg", 1, 0), chunk("qkg", 1, 1), chunk("qkg", 1, 2), chunk("o", 0, 0), chunk("o", 0, 1),
                    chunk("qkg", 0, 0), chunk("v", 0, 0), chunk("qkg", 0, 1), chunk("qkg", 0, 2), chunk("v", 0, 1)]

        CHUNKS_OF_STEP = (2, 2, 3, 3)

        def slot_bank(s, k):
            return (PROJ0[s] + k) % 2

        block = ctx.enter_context(nc.Block())

        @block.sync
        def _(sp):
            def load(q, slot):
                sp.dma_start(raw[:, slot, :], w_chunks[bass.ds(q, 1)].rearrange("a p n -> (a p) n")).then_inc(raw_in[slot], 16)

            for b in range(BATCH):
                sp.dma_start(acc[:, b * TB:(b + 1) * TB, :], x_tok[:, b * TB:(b + 1) * TB, :]).then_inc(x_in[b], 16)
                if b == 0:
                    for q in range(3):
                        load(q, q)
            for q in range(3, FIRST_CHUNKS):
                load(q, q)

            with sp.Fori(0, GROUPS) as g:
                for c in range(GROUP_CHUNKS):
                    sp.wait_ge(wlo_done, GROUP_CHUNKS * g + c + 1)
                    load(GROUP_CHUNKS * g + FIRST_CHUNKS + c, c % RAW_SLOTS)

            sp.wait_ge(table_done, 3 * HEADS)
            sp.dma_start(ar, a_router).then_inc(late_in, 16)
            sp.dma_start(base_b, b_base.rearrange("(a h) -> a h", a=1).to_broadcast([P, HID])).then_inc(again_in, 16)
            sp.dma_start(x_again, x_tok).then_inc(again_in, 16)
            for t in range(NTB):
                sp.wait_ge(result_done, t + 1)
                sp.dma_start(out_tok[:, t, :], acc[:, t, :]).then_inc(stored, 16)
            sp.wait_ge(stored, 16 * NTB)

        @block.gpsimd
        def _(pool):
            pool.iota(tanh_g[:, 0:2 * P].bitcast(mybir.dt.int32), pattern=[[-1, 2 * P]], base=0,
                      channel_multiplier=1).then_inc(diff_made, 1)
            pool.wait_ge(diff_made, 1)
            pool.tensor_copy(diff, tanh_g[:, 0:2 * P].bitcast(mybir.dt.int32)).then_inc(diff_made, 1)
            pool.wait_ge(diff_made, 2)
            pool.affine_select(out=diff, in_=diff, compare_op=ALU.is_ge, fill=-1e6, base=0,
                               pattern=[[1, 2 * P]], channel_multiplier=-1).then_inc(diff_made, 1)
            pool.memset(ident[:], 0.0).then_inc(consts, 1)
            pool.wait_ge(consts, 1)
            pool.affine_select(out=ident[:], in_=ident[:], compare_op=ALU.not_equal, fill=1.0, base=0,
                               pattern=[[-1, P]], channel_multiplier=1).then_inc(consts, 1)
            pool.memset(minus_half[:], -0.5).then_inc(consts, 1)
            pool.memset(ones[:], 1.0).then_inc(consts, 1)
            pool.memset(sum_sq[:], 0.0).then_inc(consts, 1)
            pool.memset(p_hi[:, P_AT[3]:P_AT[3] + P].bitcast(F32), 0.0).then_inc(consts, 1)
            pool.memset(p_lo[:, P_AT[3]:P_AT[3] + P].bitcast(F32), 0.0).then_inc(consts, 1)

            def power(n):
                pool.wait_ge(consts, 3)
                pool.wait_ge(pow_ready, n)
                pool.tensor_tensor(rs[:, 1, :], rs[:, 0, :], minus_half[:], ALU.pow).then_inc(pow_done, 1)

            power(1)
            pool.wait_ge(turned, NTB)
            pool.memset(acc[:], 0.0).then_inc(acc_zero, 1)

            def split_lo(hi, lo, n, slot):
                pool.wait_ge(whi_done, n + 1)
                pool.tensor_tensor(lo, raw[:, slot, :], hi.bitcast(F32), ALU.subtract).then_inc(wlo_done, 1)

            for n, (hi, lo) in enumerate(first_weights()):
                split_lo(hi, lo, n, n)

            def add_square(n, b):
                pool.wait_ge(square_done, n + 1)
                pool.wait_ge(summed, n + 5)
                pool.tensor_tensor(sum_sq[:, b, :], sum_sq[:, b, :], square[:], ALU.add).then_inc(summed, 1)

            pool.wait_ge(consts, 7)
            for _ in range(5):
                pool.sem_inc(summed, 1)

            def group(g, first=False):
                chunks = weights()
                c = 0
                for s in range(STEPS):
                    n = STEPS * g + s
                    for i in range(CHUNKS_OF_STEP[s]):
                        if i == 1 and not (first and s == 0):
                            add_square(n - 1, (s - 1) % 2)
                        hi, lo = chunks[c]
                        split_lo(hi, lo, GROUP_CHUNKS * g + FIRST_CHUNKS + c, c % RAW_SLOTS)
                        c += 1

            group(0, first=True)
            with pool.Fori(1, GROUPS) as g:
                group(g)
            add_square(STEPS * GROUPS - 1, 1)
            pool.wait_ge(again_in, 32)
            for t in range(NTB):
                pool.tensor_tensor(x_again[:, t, :], x_again[:, t, :], base_b[:], ALU.add).then_inc(xb_done, 1)
            power(2)

        @block.scalar
        def _(act):
            act.dma_start(slope[:], slopes.rearrange("(a h) -> a h", a=1).to_broadcast([P, HEADS])).then_inc(slope_in, 16)
            act.dma_start(norm[:], norm_w).then_inc(norm_in, 16)
            act.wait_ge(slope_in, 16)
            act.wait_ge(diff_made, 3)
            for i in range(2):
                act.activation(far[:, i, :], slope[:], ACT.Exp, scale=-float(P * (i + 1))).then_inc(decay_made, 1)
            for h in range(HEADS):
                act.activation(decay[:, h, :], diff, ACT.Exp, scale=slope[:, h:h + 1]).then_inc(decay_made, 1)

            def transposed_hi():
                for t in range(NTB):
                    act.wait_ge(turned, t + 1)
                    act.activation(xhi[:, :, t * P:(t + 1) * P], score[t % 2][:, :].rearrange("p (c n) -> p c n", c=KC),
                                   ACT.Copy).then_inc(xhi_done, 1)

            def split_hi(hi, slot):
                act.activation(hi, raw[:, slot, :], ACT.Copy).then_inc(whi_done, 1)

            for n, (hi, lo) in enumerate(first_weights()):
                act.wait_ge(raw_in[n], 16)
                split_hi(hi, n)
                if n == 0:
                    transposed_hi()
            act.preload_act_table_set("silu_and_others")

            def group(g, first=False):
                chunks = weights()
                c = 0
                for s in range(STEPS):
                    n = STEPS * g + s
                    h, b = s // 2, s % 2
                    slot = PROJ * g + PROJ0[s]
                    last = not (first and s == 0)

                    def weight():
                        nonlocal c
                        act.wait_ge(raw_in[c % RAW_SLOTS], 16 * (2 * g + 2 + c // RAW_SLOTS))
                        if c == 0:
                            at_least(act, proj_ready, PROJ * g)
                        if c == 3:
                            at_least(act, out_ready, NTB * g)
                        if c == 5:
                            act.wait_ge(proj_ready, PROJ * g + PROJ0[2])
                        split_hi(chunks[c][0], c % RAW_SLOTS)
                        c += 1

                    act.wait_ge(proj_ready, slot + 1)
                    at_least(act, qlo_done, n)
                    act.activation(qf[:], proj[slot_bank(s, 0)][:, :], ACT.Silu).then_inc(proj_free, 1)
                    weight()
                    at_least(act, scores_ready, TB * n)
                    act.wait_ge(proj_free, slot + 1)
                    act.activation(q_hi[:], qf[:], ACT.Copy).then_inc(qhi_done, 1)
                    if last:
                        act.wait_ge(att_ready, n)
                        at_least(act, summed, n - 1 + 5)
                        act.activation(square[:], att[:, :], ACT.Square).then_inc(square_done, 1)
                    weight()
                    if last:
                        act.wait_ge(gated_done, n)
                        if s == 1:
                            at_least(act, out_ready, NTB * g - TB)
                        if s == 2:
                            at_least(act, out_ready, NTB * g)
                        act.activation(g_hi[(s - 1) % STEPS][:], gated[:], ACT.Copy).then_inc(ghi_done, 1)
                    if s < BATCH:
                        at_least(act, att_ready, STEPS * g - 1 + s)
                        for t in range(TB + 1):
                            if t < TB:
                                act.wait_ge(proj_ready, slot + 2 + t)
                                at_least(act, vlo_done, NTB * g + s * TB + t - TB + 1)
                                act.activation(vf[t][:], proj[slot_bank(s, 1 + t)][:, 0:GH * D],
                                               ACT.Silu).then_inc(proj_free, 1)
                            if t >= 1:
                                act.wait_ge(proj_free, slot + 1 + t)
                                act.activation(v_hi[s][:, t - 1, :], vf[t - 1][:], ACT.Copy).then_inc(vhi_done, 1)
                    k_slot = 1 + (TB if s < BATCH else 0)
                    act.wait_ge(proj_ready, slot + k_slot + 1)
                    at_least(act, klo_done, n)
                    act.activation(kf[:], proj[slot_bank(s, k_slot)][:, :], ACT.Silu).then_inc(proj_free, 1)
                    if CHUNKS_OF_STEP[s] == 3:
                        weight()
                    act.wait_ge(proj_free, slot + k_slot + 1)
                    act.activation(k_hi[:], kf[:], ACT.Copy).then_inc(khi_done, 1)
                    act.wait_ge(proj_ready, slot + k_slot + 2)
                    at_least(act, gated_done, n)
                    act.activation(tanh_g[:], proj[slot_bank(s, k_slot + 1)][:, :], ACT.Tanh,
                                   scale=0.5).then_inc(proj_free, 1)
                    for j in range(TB):
                        act.wait_ge(masked, TB * n + j + 1)
                        lo = P_AT[j] + S_LEN[j] - F_LEN[j]
                        act.activation(p_hi[:, lo:lo + F_LEN[j]], pf[:, F_AT[j]:F_AT[j] + F_LEN[j]],
                                       ACT.Copy).then_inc(phi_done, 1)

            group(0, first=True)
            with act.Fori(1, GROUPS) as g:
                group(g)

            N = STEPS * GROUPS
            act.wait_ge(att_ready, N)
            act.wait_ge(summed, N - 1 + 5)
            act.activation(square[:], att[:, :], ACT.Square).then_inc(square_done, 1)
            act.wait_ge(gated_done, N)
            act.activation(g_hi[STEPS - 1][:], gated[:], ACT.Copy).then_inc(ghi_done, 1)
            act.wait_ge(route, 2)
            act.activation(sm[2], sm[1], ACT.Exp).then_inc(route_act, 1)
            for t in range(2):
                act.wait_ge(hw_turned, t + 1)
                act.activation(hw_hi[t][:], score[t][:, :], ACT.Copy).then_inc(hwhi_done, 1)

        @block.vector
        def _(dve):
            done = [0]

            def link(ins):
                done[0] += 1
                ins.then_inc(ln, 1)
                dve.wait_ge(ln, done[0])

            def refine(k):
                dve.wait_ge(pow_done, k)
                link(dve.tensor_tensor(rs[:, 2, :], rs[:, 1, :], rs[:, 1, :], ALU.mult))
                link(dve.tensor_tensor(rs[:, 3, :], rs[:, 2, :], rs[:, 0, :], ALU.mult))
                link(dve.tensor_scalar(rs[:, 2, :], rs[:, 3, :], -0.5, 1.5, ALU.mult, ALU.add))
                link(dve.tensor_tensor(rs[:, 1, :], rs[:, 1, :], rs[:, 2, :], ALU.mult))

            for t in range(NTB):
                if t % TB == 0:
                    dve.wait_ge(x_in[t // TB], 16)
                dve.bn_stats(stats[:, t, :], acc[:, t, :]).then_inc(ln, 1)
            done[0] += NTB
            dve.wait_ge(ln, done[0])
            for t in range(NTB):
                dve.bn_aggr(mean_var[:, t, :], stats[:, t, :]).then_inc(ln, 1)
            done[0] += NTB
            dve.wait_ge(ln, done[0])
            dve.tensor_scalar(rs[:, 0, :], mean_var[:, :, 1], EPS, None, ALU.add).then_inc(pow_ready, 1)
            dve.wait_ge(pow_ready, 1)
            refine(1)
            for t in range(NTB):
                dve.tensor_scalar(acc[:, t, :], acc[:, t, :], mean_var[:, t, 0:1], rs[:, 1, t:t + 1],
                                  ALU.subtract, ALU.mult).then_inc(xn_ready, 1)
            for t in range(NTB):
                dve.wait_ge(xhi_done, t + 1)
                dve.tensor_tensor(xlo[:, :, t * P:(t + 1) * P], score[t % 2][:, :].rearrange("p (c n) -> p c n", c=KC),
                                  xhi[:, :, t * P:(t + 1) * P].bitcast(F32), ALU.subtract).then_inc(xlo_done, 1)
            dve.wait_ge(decay_made, HEADS + 2)
            dve.wait_ge(norm_in, 16)
            link(dve.tensor_scalar(half_norm[:], norm[:], 0.5, None, ALU.mult))

            def finish_att(g, s):
                n = STEPS * g + s
                dve.wait_ge(square_done, n + 1)
                dve.wait_ge(gate_done, n + 1)
                at_least(dve, glo_done, n)
                dve.tensor_tensor(gated[:], att[:, :], tanh_g[:], ALU.mult).then_inc(gated_done, 1)

            def gated_lo(g, s):
                n = STEPS * g + s
                dve.wait_ge(ghi_done, n + 1)
                dve.tensor_tensor(g_lo[s][:], gated[:], g_hi[s][:].bitcast(F32), ALU.subtract).then_inc(glo_done, 1)

            def add_out(o, b):
                for t in range(TB):
                    dve.wait_ge(out_ready, o + t + 1)
                    dve.tensor_tensor(acc[:, b * TB + t, :], acc[:, b * TB + t, :], outp[t % 2][:, :],
                                      ALU.add).then_inc(acc_done, 1)

            def group(g, first=False):
                for s in range(STEPS):
                    n = STEPS * g + s
                    h, b = s // 2, s % 2
                    if b == 0:
                        head = GH * g + h
                        at_least(dve, masked, TB * n)
                        dve.tensor_copy(table[:, 0:2 * P], decay[:, bass.ds(head, 1), :].rearrange("p a n -> p (a n)")).then_inc(table_done, 1)
                        for i in range(2):
                            dve.tensor_scalar(table[:, (2 + i) * P:(3 + i) * P],
                                              decay[:, bass.ds(head, 1), P:2 * P].rearrange("p a n -> p (a n)"),
                                              far[:, i, bass.ds(head, 1)], None, ALU.mult).then_inc(table_done, 1)
                    dve.wait_ge(qhi_done, n + 1)
                    dve.tensor_tensor(q_lo[:], qf[:], q_hi[:].bitcast(F32), ALU.subtract).then_inc(qlo_done, 1)
                    if not (first and s == 0):
                        gp, sp_ = (g, s - 1) if s else (g - 1, STEPS - 1)
                        finish_att(gp, sp_)
                        gated_lo(gp, sp_)
                    if s < BATCH:
                        for t in range(TB):
                            dve.wait_ge(vhi_done, NTB * g + TB * s + t + 1)
                            dve.tensor_tensor(v_lo[s][:, t, :], vf[t][:], v_hi[s][:, t, :].bitcast(F32),
                                              ALU.subtract).then_inc(vlo_done, 1)
                    dve.wait_ge(khi_done, n + 1)
                    dve.tensor_tensor(k_lo[:], kf[:], k_hi[:].bitcast(F32), ALU.subtract).then_inc(klo_done, 1)
                    if first and s == 3:
                        dve.wait_ge(acc_zero, 1)
                    if s == 3:
                        add_out(NTB * g, 0)
                    if s == 0 and not first:
                        add_out(NTB * g - TB, 1)
                    if b == 0:
                        dve.wait_ge(table_done, 3 * (GH * g + h) + 3)
                    for j in range(TB):
                        dve.wait_ge(scores_ready, TB * n + j + 1)
                        at_least(dve, plo_done, TB * n)
                        src = S[j][:, S_LEN[j] - F_LEN[j]:S_LEN[j]]
                        dve.tensor_tensor(pf[:, F_AT[j]:F_AT[j] + F_LEN[j]], src, table[:, 0:F_LEN[j]],
                                          ALU.mult).then_inc(masked, 1)
                    dve.wait_ge(proj_free, PROJ * g + PROJ0[s] + 3 + (TB if s < BATCH else 0))
                    dve.tensor_scalar(tanh_g[:], tanh_g[:], 1.0, half_norm[:, bass.ds(GH * g + h, 1)],
                                      ALU.add, ALU.mult).then_inc(gate_done, 1)
                    for j in range(TB):
                        dve.wait_ge(phi_done, TB * n + j + 1)
                        lo = P_AT[j] + S_LEN[j] - F_LEN[j]
                        dve.tensor_tensor(p_lo[:, lo:lo + F_LEN[j]], pf[:, F_AT[j]:F_AT[j] + F_LEN[j]],
                                          p_hi[:, lo:lo + F_LEN[j]].bitcast(F32), ALU.subtract).then_inc(plo_done, 1)

            group(0, first=True)
            with dve.Fori(1, GROUPS) as g:
                group(g)

            def make_xf(t):
                if t >= 2:
                    dve.wait_ge(h_ready, t - 1)
                dve.tensor_tensor(xf[t % 2][:, :].rearrange("p (c n) -> p c n", c=KC),
                                  xhi[:, :, t * P:(t + 1) * P].bitcast(F32),
                                  xlo[:, :, t * P:(t + 1) * P].bitcast(F32), ALU.add).then_inc(xf_done, 1)

            def read_h(t):
                dve.wait_ge(h_ready, t + 1)
                dve.tensor_copy(h_keep[:, t, :], proj[t % 2][:, 0:ER]).then_inc(h_read, 1)
                dve.tensor_copy(sm[0][:, t, :], proj[t % 2][:, ER:ER + EXPERTS]).then_inc(h_read, 1)

            make_xf(0)
            make_xf(1)
            for t in range(NTB):
                read_h(t)
                if t + 2 < NTB:
                    make_xf(t + 2)
            finish_att(GROUPS - 1, STEPS - 1)
            gated_lo(GROUPS - 1, STEPS - 1)
            dve.wait_ge(h_read, 2 * NTB)

            def experts(a):
                return a.unsqueeze(2).to_broadcast([P, NTB, EXPERTS])

            link(dve.tensor_reduce(sm1[0], sm[0], AX.X, ALU.max))
            dve.tensor_tensor(sm[1], sm[0], experts(sm1[0]), ALU.subtract).then_inc(route, 2)
            add_out(NTB * GROUPS - TB, 1)
            dve.wait_ge(route_act, 1)
            link(dve.tensor_reduce(sm1[1], sm[2], AX.X, ALU.add))
            link(dve.reciprocal(sm1[2], sm1[1]))
            link(dve.tensor_tensor(sm[3], sm[2], experts(sm1[2]), ALU.mult))
            for e in range(EXPERTS):
                dve.memset(sm[4][:, :, e:e + 1], float(EXPERTS - e)).then_inc(ln, 1)
            done[0] += EXPERTS
            dve.wait_ge(ln, done[0])
            for k in range(TOP_K):
                left = 3 if k == 0 else 5
                link(dve.tensor_reduce(sm1[3 + k], sm[left], AX.X, ALU.max))
                link(dve.tensor_tensor(sm[6], sm[left], experts(sm1[3 + k]), ALU.is_equal))
                link(dve.tensor_tensor(sm[6], sm[6], sm[4], ALU.mult))
                link(dve.tensor_reduce(sm1[5], sm[6], AX.X, ALU.max))
                link(dve.tensor_tensor(sm[6], sm[4], experts(sm1[5]), ALU.is_equal))
                if k == 0:
                    link(dve.scalar_tensor_tensor(out=sm[5], in0=sm[6], scalar=-4.0,
                                                  in1=sm[3], op0=ALU.mult, op1=ALU.add))
                    link(dve.tensor_copy(sm[7], sm[6]))
                else:
                    link(dve.tensor_tensor(sm[7], sm[7], sm[6], ALU.add))
            link(dve.tensor_tensor(sm1[5], sm1[3], sm1[4], ALU.add))
            link(dve.reciprocal(sm1[6], sm1[5]))
            link(dve.scalar_tensor_tensor(out=sm[6], in0=sm[3], scalar=LORA_SCALING,
                                          in1=sm[7], op0=ALU.mult, op1=ALU.mult))
            link(dve.tensor_tensor(sm[5], sm[6], experts(sm1[6]), ALU.mult))
            for t in range(NTB):
                hv = h_keep[:, t, :].rearrange("p (e r) -> p e r", e=EXPERTS)
                dve.tensor_tensor(hv, hv, sm[5][:, t, :].unsqueeze(2).to_broadcast([P, EXPERTS, RANK]),
                                  ALU.mult).then_inc(hw_done, 1)
            for t in range(2):
                dve.wait_ge(hwhi_done, t + 1)
                dve.tensor_tensor(hw_lo[t][:], score[t][:, :], hw_hi[t][:].bitcast(F32), ALU.subtract).then_inc(hwlo_done, 1)
            dve.wait_ge(rms_ready, 1)
            dve.tensor_scalar(rs[:, 0, :], score[2][:, 0:NTB], 1.0 / (HEADS * D), EPS, ALU.mult, ALU.add).then_inc(pow_ready, 1)
            dve.wait_ge(pow_ready, 2)
            refine(2)
            for t in range(NTB):
                dve.wait_ge(xb_done, t + 1)
                dve.wait_ge(acc_done, NTB * GROUPS)
                dve.scalar_tensor_tensor(out=acc[:, t, :], in0=acc[:, t, :], scalar=rs[:, 1, t:t + 1],
                                         in1=x_again[:, t, :], op0=ALU.mult, op1=ALU.add).then_inc(part_done, 1)
            for t in range(NTB):
                dve.wait_ge(part_done, t + 1)
                dve.wait_ge(ffn_ready, t + 1)
                dve.tensor_tensor(acc[:, t, :], proj[t % 2][:, :], acc[:, t, :], ALU.add).then_inc(result_done, 1)

        @block.tensor
        def _(pe):
            def three(out_, a_hi, a_lo, b_hi, b_lo, start, stop):
                pe.matmul(out_, a_hi, b_hi, start=start, stop=False)
                pe.matmul(out_, a_hi, b_lo, start=False, stop=False)
                return pe.matmul(out_, a_lo, b_hi, start=False, stop=stop)

            pe.wait_ge(consts, 2)
            for t in range(NTB):
                pe.wait_ge(xn_ready, t + 1)
                at_least(pe, xlo_done, t - 1)
                for c in range(KC):
                    mm = pe.transpose(score[t % 2][:, c * P:(c + 1) * P], acc[:, t, c * P:(c + 1) * P], ident[:])
                mm.then_inc(turned, 1)
            pe.wait_ge(xlo_done, NTB)

            def project(g, s, h, c, k):
                b = s % 2
                slot = PROJ * g + PROJ0[s] + k
                at_least(pe, proj_free, slot - 1)
                for kc in range(KC):
                    w = slice(kc * P, (kc + 1) * P)
                    x_ = slice(b * SEQ, (b + 1) * SEQ)
                    mm = three(proj[slot_bank(s, k)][:, :], qkg_hi[h][:, c, w], qkg_lo[h][:, c, w],
                               xhi[:, kc, x_], xlo[:, kc, x_], kc == 0, kc == KC - 1)
                mm.then_inc(proj_ready, 1)

            def project_v(g, s):
                for t in range(TB):
                    slot = PROJ * g + PROJ0[s] + 1 + t
                    at_least(pe, proj_free, slot - 1)
                    tok = slice((s * TB + t) * P, (s * TB + t + 1) * P)
                    for kc in range(KC):
                        w = slice((kc % 2) * 256, (kc % 2) * 256 + 256)
                        mm = three(proj[slot_bank(s, 1 + t)][:, 0:GH * D], xhi[:, kc, tok], xlo[:, kc, tok],
                                   wv_hi[:, kc // 2, w], wv_lo[:, kc // 2, w], kc == 0, kc == KC - 1)
                    mm.then_inc(proj_ready, 1)

            def attend(g, s):
                n = STEPS * g + s
                h, b = s // 2, s % 2
                pe.wait_ge(plo_done, TB * n + TB)
                if h == 0:
                    pe.wait_ge(vlo_done, NTB * g + TB * (b + 1))
                at_least(pe, gated_done, n)
                at_least(pe, square_done, n)
                for j in range(TB):
                    e = slice(h * D, (h + 1) * D)
                    pc = slice(P_AT[j], P_AT[j] + S_LEN[j])
                    mm = three(att[:, S_FROM[j]:SEQ], v_hi[b][:, j, e], v_lo[b][:, j, e], p_hi[:, pc], p_lo[:, pc],
                               j == 0, j == TB - 1)
                mm.then_inc(att_ready, 1)

            def output(o, b, g, last_step):
                pe.wait_ge(glo_done, STEPS * g + last_step + 1)
                pe.wait_ge(wlo_done, GROUP_CHUNKS * g + FIRST_CHUNKS + 5)
                for t in range(TB):
                    at_least(pe, acc_done, o + t - 1)
                    for h in range(GH):
                        s = h * BATCH + b
                        tok = slice(t * P, (t + 1) * P)
                        mm = three(outp[t % 2][:, :], g_hi[s][:, tok], g_lo[s][:, tok], wo_hi[:, h, :], wo_lo[:, h, :],
                                   h == 0, h == GH - 1)
                    mm.then_inc(out_ready, 1)

            def scores(g, s):
                n = STEPS * g + s
                pe.wait_ge(qlo_done, n + 1)
                pe.wait_ge(klo_done, n + 1)
                at_least(pe, masked, TB * n)
                for j in range(TB):
                    key = slice(j * P, (j + 1) * P)
                    if j >= 3:
                        pe.wait_ge(masked, TB * n + j - 2)
                    mm = three(S[j], k_hi[:, key], k_lo[:, key], q_hi[:, S_FROM[j]:SEQ], q_lo[:, S_FROM[j]:SEQ],
                               True, True)
                    mm.then_inc(scores_ready, 1)

            def group(g, first=False):
                for s in range(STEPS):
                    h = s // 2
                    if s == 0:
                        pe.wait_ge(wlo_done, GROUP_CHUNKS * g + 1)
                    if s == 2:
                        pe.wait_ge(wlo_done, GROUP_CHUNKS * g + FIRST_CHUNKS + 3)
                    project(g, s, h, 0, 0)
                    if s:
                        attend(g, s - 1)
                    elif not first:
                        attend(g - 1, STEPS - 1)
                    k = 1
                    if s == 0:
                        pe.wait_ge(wlo_done, GROUP_CHUNKS * g + FIRST_CHUNKS)
                    if s < BATCH:
                        project_v(g, s)
                        k += TB
                    project(g, s, h, 1, k)
                    project(g, s, h, 2, k + 1)
                    if s == 0 and not first:
                        output(NTB * g - TB, 1, g - 1, 3)
                    if s == 3:
                        output(NTB * g, 0, g, 2)
                    scores(g, s)

            pe.wait_ge(consts, 7)
            group(0, first=True)
            with pe.Fori(1, GROUPS) as g:
                group(g)

            pe.wait_ge(late_in, 16)
            pe.wait_ge(proj_free, PROJ * GROUPS)
            for t in range(NTB):
                pe.wait_ge(xf_done, t + 1)
                if t >= 2:
                    pe.wait_ge(h_read, 2 * (t - 1))
                for kc in range(KC):
                    mm = pe.matmul(proj[t % 2][:, 0:ER + EXPERTS], xf[t % 2][:, kc * P:(kc + 1) * P], ar[:, kc, :],
                                   start=kc == 0, stop=kc == KC - 1)
                mm.then_inc(h_ready, 1)
            attend(GROUPS - 1, STEPS - 1)
            output(NTB * GROUPS - TB, 1, GROUPS - 1, 3)
            pe.wait_ge(summed, STEPS * GROUPS + 5)
            pe.wait_ge(masked, TB * STEPS * GROUPS)
            for t in range(NTB):
                mm = pe.matmul(score[2][:, t:t + 1], sum_sq[:, t // TB, (t % TB) * P:(t % TB + 1) * P], ones[:],
                               start=True, stop=True)
            mm.then_inc(rms_ready, 1)
            pe.wait_ge(wlo_done, GROUP_CHUNKS * GROUPS + FIRST_CHUNKS)

            def base(t):
                tok = slice(t * P, (t + 1) * P)
                for kc in range(KC):
                    w_hi, w_lo = (qkg_hi[0][:, kc, :], qkg_lo[0][:, kc, :]) if kc < 3 else (wv_hi[:, 0, :], wv_lo[:, 0, :])
                    three(proj[t % 2][:, :], xhi[:, kc, tok], xlo[:, kc, tok], w_hi, w_lo, kc == 0, False)

            def expert(t):
                tok = slice((t % TB) * P, (t % TB + 1) * P)
                mm = three(proj[t % 2][:, :], hw_hi[t // TB][:, tok], hw_lo[t // TB][:, tok], wv_hi[:, 1, :],
                           wv_lo[:, 1, :], False, True)
                mm.then_inc(ffn_ready, 1)

            pe.wait_ge(h_read, 2 * NTB)
            base(0)
            base(1)
            for t in range(NTB):
                pe.wait_ge(hw_done, t + 1)
                mm = pe.transpose(score[t // TB][:, (t % TB) * P:(t % TB + 1) * P], h_keep[:, t, :], ident[:])
                if t % TB == TB - 1:
                    mm.then_inc(hw_turned, 1)
            for t in range(NTB):
                pe.wait_ge(hwlo_done, t // TB + 1)
                if t >= 2:
                    pe.wait_ge(result_done, t - 1)
                    base(t)
                expert(t)


def kernel(L0_attn_hidden_states, L0_attn_qkv_w, L0_attn_out_w, L0_attn_gate_w, L0_attn_norm_w,
           L0_ffn_W_base, L0_ffn_b_base, L0_ffn_W_router, L0_ffn_A, L0_ffn_B):
    import numpy as np
    import concourse.bacc as bacc
    from concourse import mybir as mb
    from concourse.bass_utils import run_bass_kernel_spmd

    def rows(w):
        return np.asarray(w).T.reshape(KC, P, -1).transpose(1, 0, 2)

    qkv = np.asarray(L0_attn_qkv_w).reshape(HEADS, 3, D, KC, P)
    gate = np.asarray(L0_attn_gate_w).reshape(HEADS, 1, D, KC, P)
    qkg = np.concatenate([qkv[:, 0:2], gate], axis=1).transpose(0, 4, 1, 3, 2).reshape(HEADS, P, 3, KC * P)
    v = qkv[:, 2].reshape(GROUPS, GH, D, KC, P).transpose(0, 4, 3, 1, 2).reshape(GROUPS, P, 2, 512)
    o = np.asarray(L0_attn_out_w).T.reshape(HEADS, D, HID)
    base = rows(L0_ffn_W_base)
    b_t = np.asarray(L0_ffn_B).transpose(0, 2, 1).reshape(ER, HID)
    chunks = [qkg[0, :, 0], qkg[0, :, 1], qkg[0, :, 2], v[0, :, 0], v[0, :, 1]]
    for g in range(GROUPS):
        h = GH * g
        chunks += [qkg[h + 1, :, 0], qkg[h + 1, :, 1], qkg[h + 1, :, 2], o[h], o[h + 1]]
        if g < GROUPS - 1:
            chunks += [qkg[h + 2, :, 0], v[g + 1, :, 0], qkg[h + 2, :, 1], qkg[h + 2, :, 2], v[g + 1, :, 1]]
        else:
            chunks += [base[:, 0], base[:, 3], base[:, 1], base[:, 2], b_t]
    a_r = np.concatenate([rows(np.asarray(L0_ffn_A).reshape(ER, HID)), rows(L0_ffn_W_router)], axis=2)
    factor = 1.0 - 1 / (32 - 1 + 1e-5) + 1e-5
    slopes = (2.0 ** (-8.0 / HEADS * (np.arange(HEADS) + 1.0)) * factor).astype(np.float32)
    ins = {
        "x": np.asarray(L0_attn_hidden_states), "w_chunks": np.stack(chunks),
        "norm_w": np.asarray(L0_attn_norm_w).reshape(HEADS, D).T, "a_router": a_r,
        "b_base": np.asarray(L0_ffn_b_base), "slopes": slopes,
    }
    nc = bacc.Bacc("TRN2", target_bir_lowering=False, num_devices=1)
    arrays = {n: np.ascontiguousarray(a) for n, a in ins.items()}
    args = [nc.dram_tensor(n, a.shape, mb.dt.from_np(a.dtype), kind="ExternalInput").ap() for n, a in arrays.items()]
    args.append(nc.dram_tensor("out", (BATCH, SEQ, HID), F32, kind="ExternalOutput").ap())
    build(nc, *args)
    r = run_bass_kernel_spmd(nc, [arrays], core_ids=[0])
    return r.results[0]["out"]
```

```python
from contextlib import ExitStack

import concourse.bass as bass
from concourse import mybir

F32 = mybir.dt.float32
F32R = mybir.dt.float32r
ALU = mybir.AluOpType
ACT = mybir.ActivationFunctionType
AX = mybir.AxisListType

P = 128
BATCH, SEQ, HID = 2, 512, 512
HEADS, D = 32, 128
KC = HID // P
TB = SEQ // P
NTB = BATCH * TB
GH = 2
GROUPS = HEADS // GH
STEPS = GH * BATCH
EXPERTS, RANK, TOP_K = 8, 16, 2
ER = EXPERTS * RANK
LORA_SCALING = 32 / RANK
EPS = 1e-5
V_AT = (1, 1 + TB)
PROJ = 3 * STEPS + NTB
PROJ0 = (0, 3 + TB, 2 * (3 + TB), 2 * (3 + TB) + 3)
SPLIT = TB - 1
P_LEN = tuple(SEQ - P * j for j in range(TB))
P_AT = tuple(sum(P_LEN[:j]) for j in range(TB))
P_COLS = sum(P_LEN[:SPLIT])
ORDER = (3, 0, 1, 2)
FIRST_CHUNKS = 5
CONSTS = 5
RAW_SLOTS = 5
GROUP_CHUNKS = 10


SLOPES = tuple(2.0 ** (-8.0 / HEADS * (h + 1)) * (1.0 - 1 / (32 - 1 + 1e-5) + 1e-5) for h in range(HEADS))


def at_least(eng, sem, value):
    if isinstance(value, int) and value <= 0:
        return
    eng.wait_ge(sem, value)


def build(nc, x, w_chunks, norm_w, a_router, b_base, slopes, out):
    x_tok = x.rearrange("b (t p) c -> p (b t) c", p=P)
    out_tok = out.rearrange("b (t p) c -> p (b t) c", p=P)

    ctx = ExitStack()
    with ctx:
        def sb(name, shape, dt=F32):
            return ctx.enter_context(nc.sbuf_tensor(name, shape, dt))

        def bank(name):
            return ctx.enter_context(nc.psum_tensor(name, [P, 512], F32))

        def sem(name):
            return ctx.enter_context(nc.semaphore(name))

        xhi = sb("xhi", [P, KC, BATCH * SEQ], F32R)
        xlo = sb("xlo", [P, KC, BATCH * SEQ], F32R)
        acc = sb("acc", [P, NTB, HID])
        decay = sb("decay", [P, HEADS, 2 * P])
        table = sb("table", [P, SEQ])
        raw = sb("raw", [P, RAW_SLOTS, 512])
        qkg_hi = [sb(f"qkg_hi{i}", [P, 3, KC * P], F32R) for i in range(GH)]
        qkg_lo = [sb(f"qkg_lo{i}", [P, 3, KC * P], F32R) for i in range(GH)]
        wv_hi = sb("wv_hi", [P, 2, 512], F32R)
        wv_lo = sb("wv_lo", [P, 2, 512], F32R)
        wo_hi = sb("wo_hi", [P, GH, HID], F32R)
        wo_lo = sb("wo_lo", [P, GH, HID], F32R)
        qf = sb("qf", [P, SEQ])
        kf = sb("kf", [P, SEQ])
        q_hi = sb("q_hi", [P, SEQ], F32R)
        q_lo = sb("q_lo", [P, SEQ], F32R)
        k_hi = sb("k_hi", [P, SPLIT * P], F32R)
        k_lo = sb("k_lo", [P, SPLIT * P], F32R)
        vf = [sb(f"vf{i}", [P, GH * D]) for i in range(SPLIT)]
        v_hi = [sb(f"v_hi{b}", [P, SPLIT, GH * D], F32R) for b in range(BATCH)]
        v_lo = [sb(f"v_lo{b}", [P, SPLIT, GH * D], F32R) for b in range(BATCH)]
        v_last = [sb(f"v_last{b}", [P, GH * D]) for b in range(BATCH)]
        pf = sb("pf", [P, sum(P_LEN)])
        p_hi = sb("p_hi", [P, P_COLS], F32R)
        p_lo = sb("p_lo", [P, P_COLS], F32R)
        tanh_g = sb("tanh_g", [P, SEQ])
        square = sb("square", [P, SEQ])
        gated = sb("gated", [P, SEQ])
        g_hi = [sb(f"g_hi{s}", [P, SEQ], F32R) for s in range(STEPS)]
        g_lo = [sb(f"g_lo{s}", [P, SEQ], F32R) for s in range(STEPS)]
        sum_sq = sb("sum_sq", [P, BATCH, SEQ])
        ident = sb("ident", [P, P])
        ones = sb("ones", [P, 1])
        slope = sb("slope", [P, HEADS])
        far = sb("far", [P, 2, HEADS])
        norm = sb("norm", [P, HEADS])
        half_norm = sb("half_norm", [P, HEADS])
        minus_half = sb("minus_half", [P, NTB])
        stats = sb("stats", [P, NTB, 6])
        mean_var = sb("mean_var", [P, NTB, 2])
        rs = sb("rs", [P, 4, NTB])

        diff = square[:, 0:2 * P]
        free = decay[:, :, :].rearrange("p h n -> p (h n)")
        taken = [0]

        def take(*shape):
            n = 1
            for d in shape:
                n *= d
            part = free[:, taken[0]:taken[0] + n]
            taken[0] += n
            if len(shape) == 1:
                return part
            names = "abc"[:len(shape)]
            sizes = {k: d for k, d in zip(names, shape)}
            return part.rearrange(f"p ({' '.join(names)}) -> p {' '.join(names)}", **sizes)

        x_again = take(NTB, HID)
        ar = take(KC, ER + EXPERTS)
        base_b = take(HID)
        h_keep = take(NTB, ER)
        sm = [take(NTB, EXPERTS) for _ in range(8)]
        sm1 = [take(NTB) for _ in range(8)]
        xf = [qf, kf]
        hw_hi = g_hi[0:2]
        hw_lo = g_lo[0:2]

        proj = [bank(f"proj{i}") for i in range(2)]
        score = [bank(f"score{i}") for i in range(3)]
        att = bank("att")
        outp = [bank(f"outp{i}") for i in range(2)]
        S = {j: score[i % 3][:, 0:P_LEN[j]] for i, j in enumerate(ORDER)}
        ffn = [(proj + outp + [att])[t % 5] for t in range(NTB)]

        x_in = [sem(f"x_in{t}") for t in range(NTB)]
        slope_in = sem("slope_in")
        raw_in = [sem(f"raw_in{i}") for i in range(RAW_SLOTS)]
        norm_in = sem("norm_in")
        again_in = sem("again_in")
        consts = sem("consts")
        diff_made = sem("diff_made")
        decay_made = sem("decay_made")
        ln = sem("ln")
        pow_ready = sem("pow_ready")
        pow_done = sem("pow_done")
        xn_ready = sem("xn_ready")
        turned = sem("turned")
        xhi_done = sem("xhi_done")
        xlo_done = sem("xlo_done")
        acc_zero = sem("acc_zero")
        whi_done = sem("whi_done")
        wlo_done = sem("wlo_done")
        proj_ready = sem("proj_ready")
        proj_free = sem("proj_free")
        qhi_done = sem("qhi_done")
        qlo_done = sem("qlo_done")
        khi_done = sem("khi_done")
        klo_done = sem("klo_done")
        vhi_done = sem("vhi_done")
        vlo_done = sem("vlo_done")
        gate_done = sem("gate_done")
        table_done = sem("table_done")
        scores_ready = sem("scores_ready")
        masked = sem("masked")
        phi_done = sem("phi_done")
        plo_done = sem("plo_done")
        att_ready = sem("att_ready")
        gated_done = sem("gated_done")
        ghi_done = sem("ghi_done")
        glo_done = sem("glo_done")
        square_done = sem("square_done")
        summed = sem("summed")
        out_ready = sem("out_ready")
        acc_done = sem("acc_done")
        late_in = sem("late_in")
        xf_done = sem("xf_done")
        h_ready = sem("h_ready")
        h_read = sem("h_read")
        route = sem("route")
        route_act = sem("route_act")
        rms_ready = sem("rms_ready")
        hw_done = sem("hw_done")
        hw_turned = sem("hw_turned")
        hwhi_done = sem("hwhi_done")
        hwlo_done = sem("hwlo_done")
        xb_done = sem("xb_done")
        part_done = sem("part_done")
        ffn_ready = sem("ffn_ready")
        result_done = sem("result_done")
        stored = sem("stored")

        def chunk(kind, i, c):
            hi, lo = {"qkg": (qkg_hi[i], qkg_lo[i]), "v": (wv_hi, wv_lo), "o": (wo_hi, wo_lo)}[kind]
            return hi[:, c, :], lo[:, c, :]

        def first_weights():
            return [chunk("qkg", 0, 0), chunk("v", 0, 0), chunk("v", 0, 1), chunk("qkg", 0, 1), chunk("qkg", 0, 2)]

        def weights():
            return [chunk("qkg", 1, 0), chunk("qkg", 1, 1), chunk("qkg", 1, 2), chunk("o", 0, 0), chunk("o", 0, 1),
                    chunk("qkg", 0, 0), chunk("v", 0, 0), chunk("qkg", 0, 1), chunk("qkg", 0, 2), chunk("v", 0, 1)]

        CHUNKS_OF_STEP = (2, 2, 3, 3)

        def slot_bank(s, k):
            return (PROJ0[s] + k) % 2

        block = ctx.enter_context(nc.Block())

        @block.sync
        def _(sp):
            def load(q, slot):
                sp.dma_start(raw[:, slot, :], w_chunks[bass.ds(q, 1)].rearrange("a p n -> (a p) n")).then_inc(raw_in[slot], 16)

            for t in range(NTB):
                sp.dma_start(acc[:, t, :], x_tok[:, t, :]).then_inc(x_in[t], 16)
                if t == TB - 1:
                    load(0, 0)
            for q in range(1, FIRST_CHUNKS):
                load(q, q)

            with sp.Fori(0, GROUPS) as g:
                for c in range(GROUP_CHUNKS):
                    sp.wait_ge(wlo_done, GROUP_CHUNKS * g + c + 1)
                    load(GROUP_CHUNKS * g + FIRST_CHUNKS + c, c % RAW_SLOTS)

            sp.wait_ge(table_done, 3 * HEADS)
            sp.dma_start(ar, a_router).then_inc(late_in, 16)
            sp.dma_start(base_b, b_base.rearrange("(a h) -> a h", a=1).to_broadcast([P, HID])).then_inc(again_in, 16)
            sp.dma_start(x_again, x_tok).then_inc(again_in, 16)
            for t in range(NTB):
                sp.wait_ge(result_done, t + 1)
                sp.dma_start(out_tok[:, t, :], acc[:, t, :]).then_inc(stored, 16)
            sp.wait_ge(stored, 16 * NTB)

        @block.gpsimd
        def _(pool):
            pool.iota(tanh_g[:, 0:2 * P].bitcast(mybir.dt.int32), pattern=[[-1, 2 * P]], base=0,
                      channel_multiplier=1).then_inc(diff_made, 1)
            pool.wait_ge(diff_made, 1)
            pool.tensor_copy(diff, tanh_g[:, 0:2 * P].bitcast(mybir.dt.int32)).then_inc(diff_made, 1)
            pool.wait_ge(diff_made, 2)
            pool.affine_select(out=diff, in_=diff, compare_op=ALU.is_ge, fill=-1e6, base=0,
                               pattern=[[1, 2 * P]], channel_multiplier=-1).then_inc(diff_made, 1)
            pool.memset(ident[:], 0.0).then_inc(consts, 1)
            pool.wait_ge(consts, 1)
            pool.affine_select(out=ident[:], in_=ident[:], compare_op=ALU.not_equal, fill=1.0, base=0,
                               pattern=[[-1, P]], channel_multiplier=1).then_inc(consts, 1)
            pool.memset(minus_half[:], -0.5).then_inc(consts, 1)
            pool.memset(ones[:], 1.0).then_inc(consts, 1)
            pool.memset(sum_sq[:], 0.0).then_inc(consts, 1)
            def power(n, cols):
                pool.wait_ge(consts, 3)
                pool.wait_ge(pow_ready, n)
                pool.tensor_tensor(rs[:, 1, cols], rs[:, 0, cols], minus_half[:, cols], ALU.pow).then_inc(pow_done, 1)

            def split_lo(hi, lo, n, slot):
                pool.wait_ge(whi_done, n + 1)
                pool.tensor_tensor(lo, raw[:, slot, :], hi.bitcast(F32), ALU.subtract).then_inc(wlo_done, 1)

            for n, (hi, lo) in enumerate(first_weights()):
                if n < BATCH:
                    power(n + 1, slice(n * TB, (n + 1) * TB))
                pool.wait_ge(raw_in[n], 16)
                pool.tensor_copy(hi, raw[:, n, :]).then_inc(whi_done, 1)
                split_lo(hi, lo, n, n)
            pool.wait_ge(turned, NTB)
            pool.memset(acc[:], 0.0).then_inc(acc_zero, 1)

            def add_square(n, b):
                pool.wait_ge(square_done, n + 1)
                at_least(pool, summed, n)
                pool.tensor_tensor(sum_sq[:, b, :], sum_sq[:, b, :], square[:], ALU.add).then_inc(summed, 1)

            pool.wait_ge(consts, CONSTS)

            def group(g, first=False):
                chunks = weights()
                c = 0
                for s in range(STEPS):
                    n = STEPS * g + s
                    for i in range(CHUNKS_OF_STEP[s]):
                        if i == 1 and not (first and s == 0):
                            add_square(n - 1, (s - 1) % 2)
                        hi, lo = chunks[c]
                        split_lo(hi, lo, GROUP_CHUNKS * g + FIRST_CHUNKS + c, c % RAW_SLOTS)
                        c += 1

            group(0, first=True)
            with pool.Fori(1, GROUPS) as g:
                group(g)
            add_square(STEPS * GROUPS - 1, 1)
            pool.wait_ge(again_in, 32)
            for t in range(NTB):
                pool.tensor_tensor(x_again[:, t, :], x_again[:, t, :], base_b[:], ALU.add).then_inc(xb_done, 1)
            power(3, slice(0, NTB))

        @block.scalar
        def _(act):
            act.dma_start(slope[:], slopes.rearrange("(a h) -> a h", a=1).to_broadcast([P, HEADS])).then_inc(slope_in, 16)
            act.dma_start(norm[:], norm_w).then_inc(norm_in, 16)
            act.wait_ge(slope_in, 16)
            act.wait_ge(diff_made, 3)
            for i in range(2):
                act.activation(far[:, i, :], slope[:], ACT.Exp, scale=-float(P * (i + 1))).then_inc(decay_made, 1)
            def decays(heads):
                for h in heads:
                    act.activation(decay[:, h, :], diff, ACT.Exp, scale=SLOPES[h]).then_inc(decay_made, 1)

            def transposed_hi(b):
                for t in range(b * TB, (b + 1) * TB):
                    act.wait_ge(turned, t + 1)
                    act.activation(xhi[:, :, t * P:(t + 1) * P], score[t % 2][:, :].rearrange("p (c n) -> p c n", c=KC),
                                   ACT.Copy).then_inc(xhi_done, 1)

            decays(range(20))
            transposed_hi(0)
            decays(range(20, HEADS))
            transposed_hi(1)

            def split_hi(hi, slot):
                act.activation(hi, raw[:, slot, :], ACT.Copy).then_inc(whi_done, 1)

            act.preload_act_table_set("silu_and_others")

            def group(g, first=False):
                chunks = weights()
                c = 0
                for s in range(STEPS):
                    n = STEPS * g + s
                    h, b = s // 2, s % 2
                    slot = PROJ * g + PROJ0[s]
                    last = not (first and s == 0)

                    def weight():
                        nonlocal c
                        act.wait_ge(raw_in[c % RAW_SLOTS], 16 * (2 * g + 2 + c // RAW_SLOTS))
                        if c == 0:
                            at_least(act, proj_ready, PROJ * g)
                            if first:
                                act.wait_ge(wlo_done, FIRST_CHUNKS)
                        if c == 3:
                            at_least(act, out_ready, NTB * g)
                        if c == 5:
                            act.wait_ge(proj_ready, PROJ * g + PROJ0[2])
                        split_hi(chunks[c][0], c % RAW_SLOTS)
                        c += 1

                    act.wait_ge(proj_ready, slot + 1)
                    at_least(act, scores_ready, TB * n)
                    act.activation(qf[:], proj[slot_bank(s, 0)][:, :], ACT.Silu).then_inc(proj_free, 1)
                    weight()
                    act.wait_ge(proj_free, slot + 1)
                    act.activation(q_hi[:], qf[:], ACT.Copy).then_inc(qhi_done, 1)
                    if last:
                        act.wait_ge(att_ready, n)
                        at_least(act, summed, n - 1)
                        act.activation(square[:], att[:, :], ACT.Square).then_inc(square_done, 1)
                    weight()
                    if last:
                        act.wait_ge(gated_done, n)
                        if s == 1:
                            at_least(act, out_ready, NTB * g - TB)
                        if s == 2:
                            at_least(act, out_ready, NTB * g)
                        act.activation(g_hi[(s - 1) % STEPS][:], gated[:], ACT.Copy).then_inc(ghi_done, 1)
                    if s < BATCH:
                        at_least(act, att_ready, STEPS * g - 1 + s)
                        for t in range(TB + 1):
                            if t < TB:
                                act.wait_ge(proj_ready, slot + 2 + t)
                                if t < SPLIT:
                                    at_least(act, vlo_done, SPLIT * (BATCH * g + s - 1) + t + 1)
                                act.activation(vf[t][:] if t < SPLIT else v_last[s][:],
                                               proj[slot_bank(s, 1 + t)][:, 0:GH * D], ACT.Silu).then_inc(proj_free, 1)
                            if 1 <= t <= SPLIT:
                                act.wait_ge(proj_free, slot + 1 + t)
                                act.activation(v_hi[s][:, t - 1, :], vf[t - 1][:], ACT.Copy).then_inc(vhi_done, 1)
                    k_slot = 1 + (TB if s < BATCH else 0)
                    act.wait_ge(proj_ready, slot + k_slot + 1)
                    act.activation(kf[:], proj[slot_bank(s, k_slot)][:, :], ACT.Silu).then_inc(proj_free, 1)
                    if CHUNKS_OF_STEP[s] == 3:
                        weight()
                    act.wait_ge(proj_free, slot + k_slot + 1)
                    act.activation(k_hi[:], kf[:, 0:SPLIT * P], ACT.Copy).then_inc(khi_done, 1)
                    act.wait_ge(proj_ready, slot + k_slot + 2)
                    at_least(act, gated_done, n)
                    act.activation(tanh_g[:], proj[slot_bank(s, k_slot + 1)][:, :], ACT.Tanh,
                                   scale=0.5).then_inc(proj_free, 1)
                    for j in range(SPLIT):
                        act.wait_ge(masked, TB * n + ORDER.index(j) + 1)
                        cols = slice(P_AT[j], P_AT[j] + P_LEN[j])
                        act.activation(p_hi[:, cols], pf[:, cols], ACT.Copy).then_inc(phi_done, 1)

            group(0, first=True)
            with act.Fori(1, GROUPS) as g:
                group(g)

            N = STEPS * GROUPS
            act.wait_ge(att_ready, N)
            act.wait_ge(summed, N - 1)
            act.activation(square[:], att[:, :], ACT.Square).then_inc(square_done, 1)
            act.wait_ge(gated_done, N)
            act.activation(g_hi[STEPS - 1][:], gated[:], ACT.Copy).then_inc(ghi_done, 1)
            act.wait_ge(route, 2)
            act.activation(sm[2], sm[1], ACT.Exp).then_inc(route_act, 1)
            for t in range(2):
                act.wait_ge(hw_turned, t + 1)
                act.activation(hw_hi[t][:], score[t][:, :], ACT.Copy).then_inc(hwhi_done, 1)

        @block.vector
        def _(dve):
            done = [0]

            def link(ins):
                done[0] += 1
                ins.then_inc(ln, 1)
                dve.wait_ge(ln, done[0])

            def refine(k, cols):
                v, y, a, b = (rs[:, i, cols] for i in range(4))
                dve.wait_ge(pow_done, k)
                link(dve.tensor_tensor(a, y, y, ALU.mult))
                link(dve.tensor_tensor(b, a, v, ALU.mult))
                link(dve.tensor_scalar(a, b, -0.5, 1.5, ALU.mult, ALU.add))
                link(dve.tensor_tensor(y, y, a, ALU.mult))

            def statistics(b):
                for t in range(b * TB, (b + 1) * TB):
                    dve.wait_ge(x_in[t], 16)
                    dve.bn_stats(stats[:, t, :], acc[:, t, :]).then_inc(ln, 1)
                done[0] += TB
                dve.wait_ge(ln, done[0])
                for t in range(b * TB, (b + 1) * TB):
                    dve.bn_aggr(mean_var[:, t, :], stats[:, t, :]).then_inc(ln, 1)
                done[0] += TB
                dve.wait_ge(ln, done[0])
                cols = slice(b * TB, (b + 1) * TB)
                dve.tensor_scalar(rs[:, 0, cols], mean_var[:, cols, 1], EPS, None, ALU.add).then_inc(pow_ready, 1)

            def normalise(b):
                dve.wait_ge(pow_ready, b + 1)
                refine(b + 1, slice(b * TB, (b + 1) * TB))
                for t in range(b * TB, (b + 1) * TB):
                    dve.tensor_scalar(acc[:, t, :], acc[:, t, :], mean_var[:, t, 0:1], rs[:, 1, t:t + 1],
                                      ALU.subtract, ALU.mult).then_inc(xn_ready, 1)

            def transposed_lo(b):
                for t in range(b * TB, (b + 1) * TB):
                    dve.wait_ge(xhi_done, t + 1)
                    dve.tensor_tensor(xlo[:, :, t * P:(t + 1) * P],
                                      score[t % 2][:, :].rearrange("p (c n) -> p c n", c=KC),
                                      xhi[:, :, t * P:(t + 1) * P].bitcast(F32), ALU.subtract).then_inc(xlo_done, 1)

            statistics(0)
            normalise(0)
            transposed_lo(0)
            statistics(1)
            normalise(1)
            transposed_lo(1)
            dve.wait_ge(decay_made, HEADS + 2)
            dve.wait_ge(norm_in, 16)
            link(dve.tensor_scalar(half_norm[:], norm[:], 0.5, None, ALU.mult))

            def finish_att(g, s):
                n = STEPS * g + s
                dve.wait_ge(square_done, n + 1)
                dve.wait_ge(gate_done, n + 1)
                at_least(dve, glo_done, n)
                dve.tensor_tensor(gated[:], att[:, :], tanh_g[:], ALU.mult).then_inc(gated_done, 1)

            def gated_lo(g, s):
                n = STEPS * g + s
                dve.wait_ge(ghi_done, n + 1)
                dve.tensor_tensor(g_lo[s][:], gated[:], g_hi[s][:].bitcast(F32), ALU.subtract).then_inc(glo_done, 1)

            def add_out(o, b):
                for t in range(TB):
                    dve.wait_ge(out_ready, o + t + 1)
                    dve.tensor_tensor(acc[:, b * TB + t, :], acc[:, b * TB + t, :], outp[t % 2][:, :],
                                      ALU.add).then_inc(acc_done, 1)

            def group(g, first=False):
                for s in range(STEPS):
                    n = STEPS * g + s
                    h, b = s // 2, s % 2
                    if b == 0:
                        head = GH * g + h
                        at_least(dve, masked, TB * n)
                        dve.tensor_copy(table[:, 0:2 * P], decay[:, bass.ds(head, 1), :].rearrange("p a n -> p (a n)")).then_inc(table_done, 1)
                        for i in range(2):
                            dve.tensor_scalar(table[:, (2 + i) * P:(3 + i) * P],
                                              decay[:, bass.ds(head, 1), P:2 * P].rearrange("p a n -> p (a n)"),
                                              far[:, i, bass.ds(head, 1)], None, ALU.mult).then_inc(table_done, 1)
                    dve.wait_ge(qhi_done, n + 1)
                    dve.tensor_tensor(q_lo[:], qf[:], q_hi[:].bitcast(F32), ALU.subtract).then_inc(qlo_done, 1)
                    if not (first and s == 0):
                        gp, sp_ = (g, s - 1) if s else (g - 1, STEPS - 1)
                        finish_att(gp, sp_)
                        gated_lo(gp, sp_)
                    if s < BATCH:
                        for t in range(SPLIT):
                            dve.wait_ge(vhi_done, SPLIT * (BATCH * g + s) + t + 1)
                            dve.tensor_tensor(v_lo[s][:, t, :], vf[t][:], v_hi[s][:, t, :].bitcast(F32),
                                              ALU.subtract).then_inc(vlo_done, 1)
                    dve.wait_ge(khi_done, n + 1)
                    dve.tensor_tensor(k_lo[:], kf[:, 0:SPLIT * P], k_hi[:].bitcast(F32), ALU.subtract).then_inc(klo_done, 1)
                    if first and s == 3:
                        dve.wait_ge(acc_zero, 1)
                    if s == 3:
                        add_out(NTB * g, 0)
                    if s == 0 and not first:
                        add_out(NTB * g - TB, 1)
                    if b == 0:
                        dve.wait_ge(table_done, 3 * (GH * g + h) + 3)
                    for i, j in enumerate(ORDER):
                        dve.wait_ge(scores_ready, TB * n + i + 1)
                        at_least(dve, plo_done, SPLIT * n)
                        dve.tensor_tensor(pf[:, P_AT[j]:P_AT[j] + P_LEN[j]], S[j], table[:, 0:P_LEN[j]],
                                          ALU.mult).then_inc(masked, 1)
                    dve.wait_ge(proj_free, PROJ * g + PROJ0[s] + 3 + (TB if s < BATCH else 0))
                    dve.tensor_scalar(tanh_g[:], tanh_g[:], 1.0, half_norm[:, bass.ds(GH * g + h, 1)],
                                      ALU.add, ALU.mult).then_inc(gate_done, 1)
                    for j in range(SPLIT):
                        dve.wait_ge(phi_done, SPLIT * n + j + 1)
                        cols = slice(P_AT[j], P_AT[j] + P_LEN[j])
                        dve.tensor_tensor(p_lo[:, cols], pf[:, cols], p_hi[:, cols].bitcast(F32),
                                          ALU.subtract).then_inc(plo_done, 1)

            group(0, first=True)
            with dve.Fori(1, GROUPS) as g:
                group(g)

            def make_xf(t):
                if t >= 2:
                    dve.wait_ge(h_ready, t - 1)
                dve.tensor_tensor(xf[t % 2][:, :].rearrange("p (c n) -> p c n", c=KC),
                                  xhi[:, :, t * P:(t + 1) * P].bitcast(F32),
                                  xlo[:, :, t * P:(t + 1) * P].bitcast(F32), ALU.add).then_inc(xf_done, 1)

            def read_h(t):
                dve.wait_ge(h_ready, t + 1)
                dve.tensor_copy(h_keep[:, t, :], proj[t % 2][:, 0:ER]).then_inc(h_read, 1)
                dve.tensor_copy(sm[0][:, t, :], proj[t % 2][:, ER:ER + EXPERTS]).then_inc(h_read, 1)

            make_xf(0)
            make_xf(1)
            for t in range(NTB):
                read_h(t)
                if t + 2 < NTB:
                    make_xf(t + 2)
            dve.wait_ge(h_read, 2 * NTB)

            def experts(a):
                return a.unsqueeze(2).to_broadcast([P, NTB, EXPERTS])

            link(dve.tensor_reduce(sm1[0], sm[0], AX.X, ALU.max))
            dve.tensor_tensor(sm[1], sm[0], experts(sm1[0]), ALU.subtract).then_inc(route, 2)
            finish_att(GROUPS - 1, STEPS - 1)
            gated_lo(GROUPS - 1, STEPS - 1)
            dve.wait_ge(route_act, 1)
            link(dve.tensor_reduce(sm1[1], sm[2], AX.X, ALU.add))
            link(dve.reciprocal(sm1[2], sm1[1]))
            link(dve.tensor_tensor(sm[3], sm[2], experts(sm1[2]), ALU.mult))
            for e in range(EXPERTS):
                dve.memset(sm[4][:, :, e:e + 1], float(EXPERTS - e)).then_inc(ln, 1)
            done[0] += EXPERTS
            dve.wait_ge(ln, done[0])
            for k in range(TOP_K):
                left = 3 if k == 0 else 5
                link(dve.tensor_reduce(sm1[3 + k], sm[left], AX.X, ALU.max))
                link(dve.tensor_tensor(sm[6], sm[left], experts(sm1[3 + k]), ALU.is_equal))
                link(dve.tensor_tensor(sm[6], sm[6], sm[4], ALU.mult))
                link(dve.tensor_reduce(sm1[5], sm[6], AX.X, ALU.max))
                link(dve.tensor_tensor(sm[6], sm[4], experts(sm1[5]), ALU.is_equal))
                if k == 0:
                    link(dve.scalar_tensor_tensor(out=sm[5], in0=sm[6], scalar=-4.0,
                                                  in1=sm[3], op0=ALU.mult, op1=ALU.add))
                    link(dve.tensor_copy(sm[7], sm[6]))
                else:
                    link(dve.tensor_tensor(sm[7], sm[7], sm[6], ALU.add))
            link(dve.tensor_tensor(sm1[5], sm1[3], sm1[4], ALU.add))
            link(dve.reciprocal(sm1[6], sm1[5]))
            link(dve.scalar_tensor_tensor(out=sm[6], in0=sm[3], scalar=LORA_SCALING,
                                          in1=sm[7], op0=ALU.mult, op1=ALU.mult))
            link(dve.tensor_tensor(sm[5], sm[6], experts(sm1[6]), ALU.mult))
            for t in range(NTB):
                hv = h_keep[:, t, :].rearrange("p (e r) -> p e r", e=EXPERTS)
                dve.tensor_tensor(hv, hv, sm[5][:, t, :].unsqueeze(2).to_broadcast([P, EXPERTS, RANK]),
                                  ALU.mult).then_inc(hw_done, 1)
            add_out(NTB * GROUPS - TB, 1)
            for t in range(2):
                dve.wait_ge(hwhi_done, t + 1)
                dve.tensor_tensor(hw_lo[t][:], score[t][:, :], hw_hi[t][:].bitcast(F32), ALU.subtract).then_inc(hwlo_done, 1)
            dve.wait_ge(rms_ready, 1)
            dve.tensor_scalar(rs[:, 0, :], score[2][:, 0:NTB], 1.0 / (HEADS * D), EPS, ALU.mult, ALU.add).then_inc(pow_ready, 1)
            dve.wait_ge(pow_ready, 3)
            refine(3, slice(0, NTB))
            dve.wait_ge(acc_done, NTB * GROUPS)
            for t in range(NTB):
                dve.wait_ge(xb_done, t + 1)
                dve.scalar_tensor_tensor(out=acc[:, t, :], in0=acc[:, t, :], scalar=rs[:, 1, t:t + 1],
                                         in1=x_again[:, t, :], op0=ALU.mult, op1=ALU.add).then_inc(part_done, 1)
            for t in range(NTB):
                dve.wait_ge(part_done, t + 1)
                dve.wait_ge(ffn_ready, t + 1)
                dve.tensor_tensor(acc[:, t, :], ffn[t][:, :], acc[:, t, :], ALU.add).then_inc(result_done, 1)

        @block.tensor
        def _(pe):
            def three(out_, a_hi, a_lo, b_hi, b_lo, start, stop):
                pe.matmul(out_, a_hi, b_hi, start=start, stop=False)
                pe.matmul(out_, a_hi, b_lo, start=False, stop=False)
                return pe.matmul(out_, a_lo, b_hi, start=False, stop=stop)

            def transposes(b):
                for t in range(b * TB, (b + 1) * TB):
                    pe.wait_ge(xn_ready, t + 1)
                    at_least(pe, xlo_done, t - 1)
                    for c in range(KC):
                        mm = pe.transpose(score[t % 2][:, c * P:(c + 1) * P], acc[:, t, c * P:(c + 1) * P], ident[:])
                    mm.then_inc(turned, 1)

            def project(g, s, h, c, k):
                b = s % 2
                slot = PROJ * g + PROJ0[s] + k
                at_least(pe, proj_free, slot - 1)
                for kc in range(KC):
                    w = slice(kc * P, (kc + 1) * P)
                    x_ = slice(b * SEQ, (b + 1) * SEQ)
                    mm = three(proj[slot_bank(s, k)][:, :], qkg_hi[h][:, c, w], qkg_lo[h][:, c, w],
                               xhi[:, kc, x_], xlo[:, kc, x_], kc == 0, kc == KC - 1)
                mm.then_inc(proj_ready, 1)

            def project_v(g, s):
                for t in range(TB):
                    slot = PROJ * g + PROJ0[s] + 1 + t
                    at_least(pe, proj_free, slot - 1)
                    tok = slice((s * TB + t) * P, (s * TB + t + 1) * P)
                    for kc in range(KC):
                        w = slice((kc % 2) * 256, (kc % 2) * 256 + 256)
                        mm = three(proj[slot_bank(s, 1 + t)][:, 0:GH * D], xhi[:, kc, tok], xlo[:, kc, tok],
                                   wv_hi[:, kc // 2, w], wv_lo[:, kc // 2, w], kc == 0, kc == KC - 1)
                    mm.then_inc(proj_ready, 1)

            def attend(g, s):
                n = STEPS * g + s
                h, b = s // 2, s % 2
                pe.wait_ge(plo_done, SPLIT * (n + 1))
                if h == 0:
                    pe.wait_ge(vlo_done, SPLIT * (BATCH * g + b + 1))
                at_least(pe, gated_done, n)
                e = slice(h * D, (h + 1) * D)
                for j in range(SPLIT):
                    cols = slice(P_AT[j], P_AT[j] + P_LEN[j])
                    three(att[:, j * P:SEQ], v_hi[b][:, j, e], v_lo[b][:, j, e], p_hi[:, cols], p_lo[:, cols],
                          j == 0, False)
                pe.matmul(att[:, SPLIT * P:SEQ], v_last[b][:, e], pf[:, P_AT[SPLIT]:P_AT[SPLIT] + P],
                          start=False, stop=True).then_inc(att_ready, 1)

            def output(o, b, g, last_step):
                pe.wait_ge(glo_done, STEPS * g + last_step + 1)
                pe.wait_ge(wlo_done, GROUP_CHUNKS * g + FIRST_CHUNKS + 5)
                for t in range(TB):
                    at_least(pe, acc_done, o + t - 1)
                    for h in range(GH):
                        s = h * BATCH + b
                        tok = slice(t * P, (t + 1) * P)
                        mm = three(outp[t % 2][:, :], g_hi[s][:, tok], g_lo[s][:, tok], wo_hi[:, h, :], wo_lo[:, h, :],
                                   h == 0, h == GH - 1)
                    mm.then_inc(out_ready, 1)

            def scores(g, s):
                n = STEPS * g + s
                pe.wait_ge(klo_done, n + 1)
                for i, j in enumerate(ORDER):
                    key = slice(j * P, (j + 1) * P)
                    if i == 3:
                        pe.wait_ge(masked, TB * n + 1)
                    if j == SPLIT:
                        mm = pe.matmul(S[j], kf[:, key], qf[:, key], start=True, stop=True)
                    else:
                        mm = three(S[j], k_hi[:, key], k_lo[:, key], q_hi[:, j * P:SEQ], q_lo[:, j * P:SEQ], True, True)
                    mm.then_inc(scores_ready, 1)

            def group(g, first=False):
                for s in range(STEPS):
                    h = s // 2
                    if s == 0:
                        pe.wait_ge(wlo_done, GROUP_CHUNKS * g + 1)
                    if s == 2:
                        pe.wait_ge(wlo_done, GROUP_CHUNKS * g + FIRST_CHUNKS + 3)
                    project(g, s, h, 0, 0)
                    if s:
                        attend(g, s - 1)
                    elif not first:
                        attend(g - 1, STEPS - 1)
                    else:
                        transposes(1)
                    k = 1
                    if s == 0:
                        pe.wait_ge(wlo_done, 3 if first else GROUP_CHUNKS * g + FIRST_CHUNKS)
                    if s < BATCH:
                        project_v(g, s)
                        k += TB
                    if first and s == 0:
                        pe.wait_ge(wlo_done, FIRST_CHUNKS)
                    if first and s == 1:
                        pe.wait_ge(xlo_done, NTB)
                    project(g, s, h, 1, k)
                    project(g, s, h, 2, k + 1)
                    if s == 0 and not first:
                        output(NTB * g - TB, 1, g - 1, 3)
                    if s == 3:
                        output(NTB * g, 0, g, 2)
                    scores(g, s)

            pe.wait_ge(consts, CONSTS)
            transposes(0)
            pe.wait_ge(xlo_done, TB)
            group(0, first=True)
            with pe.Fori(1, GROUPS) as g:
                group(g)

            pe.wait_ge(late_in, 16)
            pe.wait_ge(proj_free, PROJ * GROUPS)
            for t in range(NTB):
                pe.wait_ge(xf_done, t + 1)
                if t >= 2:
                    pe.wait_ge(h_read, 2 * (t - 1))
                for kc in range(KC):
                    mm = pe.matmul(proj[t % 2][:, 0:ER + EXPERTS], xf[t % 2][:, kc * P:(kc + 1) * P], ar[:, kc, :],
                                   start=kc == 0, stop=kc == KC - 1)
                mm.then_inc(h_ready, 1)
            attend(GROUPS - 1, STEPS - 1)
            pe.wait_ge(wlo_done, GROUP_CHUNKS * GROUPS + FIRST_CHUNKS)
            pe.wait_ge(h_read, 2 * NTB)

            def base(t):
                tok = slice(t * P, (t + 1) * P)
                for kc in range(KC):
                    w_hi, w_lo = (qkg_hi[0][:, kc, :], qkg_lo[0][:, kc, :]) if kc < 3 else (wv_hi[:, 0, :], wv_lo[:, 0, :])
                    three(ffn[t][:, :], xhi[:, kc, tok], xlo[:, kc, tok], w_hi, w_lo, kc == 0, False)

            def expert(t):
                tok = slice((t % TB) * P, (t % TB + 1) * P)
                mm = three(ffn[t][:, :], hw_hi[t // TB][:, tok], hw_lo[t // TB][:, tok], wv_hi[:, 1, :],
                           wv_lo[:, 1, :], False, True)
                mm.then_inc(ffn_ready, 1)

            base(0)
            base(1)
            output(NTB * GROUPS - TB, 1, GROUPS - 1, 3)
            pe.wait_ge(summed, STEPS * GROUPS)
            for t in range(NTB):
                mm = pe.matmul(score[2][:, t:t + 1], sum_sq[:, t // TB, (t % TB) * P:(t % TB + 1) * P], ones[:],
                               start=True, stop=True)
            mm.then_inc(rms_ready, 1)
            for t in range(NTB):
                pe.wait_ge(hw_done, t + 1)
                mm = pe.transpose(score[t // TB][:, (t % TB) * P:(t % TB + 1) * P], h_keep[:, t, :], ident[:])
                if t % TB == TB - 1:
                    mm.then_inc(hw_turned, 1)
            pe.wait_ge(gated_done, STEPS * GROUPS)
            pe.wait_ge(acc_done, NTB * GROUPS)
            for t in range(2, 5):
                base(t)
            for t in range(NTB):
                pe.wait_ge(hwlo_done, t // TB + 1)
                if t >= 5:
                    pe.wait_ge(result_done, t - 4)
                    base(t)
                expert(t)


def kernel(L0_attn_hidden_states, L0_attn_qkv_w, L0_attn_out_w, L0_attn_gate_w, L0_attn_norm_w,
           L0_ffn_W_base, L0_ffn_b_base, L0_ffn_W_router, L0_ffn_A, L0_ffn_B):
    import numpy as np
    import concourse.bacc as bacc
    from concourse import mybir as mb
    from concourse.bass_utils import run_bass_kernel_spmd

    def rows(w):
        return np.asarray(w).T.reshape(KC, P, -1).transpose(1, 0, 2)

    qkv = np.asarray(L0_attn_qkv_w).reshape(HEADS, 3, D, KC, P)
    gate = np.asarray(L0_attn_gate_w).reshape(HEADS, 1, D, KC, P)
    qkg = np.concatenate([qkv[:, 0:2], gate], axis=1).transpose(0, 4, 1, 3, 2).reshape(HEADS, P, 3, KC * P)
    v = qkv[:, 2].reshape(GROUPS, GH, D, KC, P).transpose(0, 4, 3, 1, 2).reshape(GROUPS, P, 2, 512)
    o = np.asarray(L0_attn_out_w).T.reshape(HEADS, D, HID)
    base = rows(L0_ffn_W_base)
    b_t = np.asarray(L0_ffn_B).transpose(0, 2, 1).reshape(ER, HID)
    chunks = [qkg[0, :, 0], v[0, :, 0], v[0, :, 1], qkg[0, :, 1], qkg[0, :, 2]]
    for g in range(GROUPS):
        h = GH * g
        chunks += [qkg[h + 1, :, 0], qkg[h + 1, :, 1], qkg[h + 1, :, 2], o[h], o[h + 1]]
        if g < GROUPS - 1:
            chunks += [qkg[h + 2, :, 0], v[g + 1, :, 0], qkg[h + 2, :, 1], qkg[h + 2, :, 2], v[g + 1, :, 1]]
        else:
            chunks += [base[:, 0], base[:, 3], base[:, 1], base[:, 2], b_t]
    a_r = np.concatenate([rows(np.asarray(L0_ffn_A).reshape(ER, HID)), rows(L0_ffn_W_router)], axis=2)
    ins = {
        "x": np.asarray(L0_attn_hidden_states), "w_chunks": np.stack(chunks),
        "norm_w": np.asarray(L0_attn_norm_w).reshape(HEADS, D).T, "a_router": a_r,
        "b_base": np.asarray(L0_ffn_b_base), "slopes": np.array(SLOPES, np.float32),
    }
    nc = bacc.Bacc("TRN2", target_bir_lowering=False, num_devices=1)
    arrays = {n: np.ascontiguousarray(a) for n, a in ins.items()}
    args = [nc.dram_tensor(n, a.shape, mb.dt.from_np(a.dtype), kind="ExternalInput").ap() for n, a in arrays.items()]
    args.append(nc.dram_tensor("out", (BATCH, SEQ, HID), F32, kind="ExternalOutput").ap())
    build(nc, *args)
    r = run_bass_kernel_spmd(nc, [arrays], core_ids=[0])
    return r.results[0]["out"]
```

```python
from contextlib import ExitStack

import concourse.bass as bass
from concourse import mybir

F32 = mybir.dt.float32
F32R = mybir.dt.float32r
ALU = mybir.AluOpType
ACT = mybir.ActivationFunctionType
AX = mybir.AxisListType

P = 128
BATCH, SEQ, HID = 2, 512, 512
HEADS, D = 32, 128
KC = HID // P
TB = SEQ // P
NTB = BATCH * TB
GH = 2
GROUPS = HEADS // GH
STEPS = GH * BATCH
EXPERTS, RANK, TOP_K = 8, 16, 2
ER = EXPERTS * RANK
LORA_SCALING = 32 / RANK
EPS = 1e-5
PROJ = 3 * STEPS + NTB
PROJ0 = (0, 3 + TB, 2 * (3 + TB), 2 * (3 + TB) + 3)
SPLIT = TB - 1
P_LEN = tuple(SEQ - P * j for j in range(TB))
P_AT = tuple(sum(P_LEN[:j]) for j in range(TB))
P_COLS = sum(P_LEN[:SPLIT])
ORDER = (3, 0, 1, 2)
FIRST_CHUNKS = 5
GROUP_CHUNKS = 10
CHUNKS_OF_STEP = (2, 2, 3, 3)
RAW_SLOTS = 5
CONSTS = 5
EARLY_HEADS = 26


SLOPES = tuple(2.0 ** (-8.0 / HEADS * (h + 1)) * (1.0 - 1 / (32 - 1 + 1e-5) + 1e-5) for h in range(HEADS))


def at_least(eng, sem, value):
    if isinstance(value, int) and value <= 0:
        return
    eng.wait_ge(sem, value)


def build(nc, x, w_chunks, norm_w, a_router, b_base, slopes, out):
    x_tok = x.rearrange("b (t p) c -> p (b t) c", p=P)
    out_tok = out.rearrange("b (t p) c -> p (b t) c", p=P)

    ctx = ExitStack()
    with ctx:
        def sb(name, shape, dt=F32):
            return ctx.enter_context(nc.sbuf_tensor(name, shape, dt))

        def bank(name):
            return ctx.enter_context(nc.psum_tensor(name, [P, 512], F32))

        def sem(name):
            return ctx.enter_context(nc.semaphore(name))

        xhi = sb("xhi", [P, KC, BATCH * SEQ], F32R)
        xlo = sb("xlo", [P, KC, BATCH * SEQ], F32R)
        acc = sb("acc", [P, NTB, HID])
        decay = sb("decay", [P, HEADS, 2 * P])
        table = sb("table", [P, SEQ])
        raw = sb("raw", [P, RAW_SLOTS, 512])
        qkg_hi = [sb(f"qkg_hi{i}", [P, 3, KC * P], F32R) for i in range(GH)]
        qkg_lo = [sb(f"qkg_lo{i}", [P, 3, KC * P], F32R) for i in range(GH)]
        wv_hi = sb("wv_hi", [P, 2, 512], F32R)
        wv_lo = sb("wv_lo", [P, 2, 512], F32R)
        wo_hi = sb("wo_hi", [P, GH, HID], F32R)
        wo_lo = sb("wo_lo", [P, GH, HID], F32R)
        qf = sb("qf", [P, SEQ])
        kf = sb("kf", [P, SEQ])
        q_hi = sb("q_hi", [P, SEQ], F32R)
        q_lo = sb("q_lo", [P, SEQ], F32R)
        k_hi = sb("k_hi", [P, SPLIT * P], F32R)
        k_lo = sb("k_lo", [P, SPLIT * P], F32R)
        vf = [sb(f"vf{i}", [P, GH * D]) for i in range(SPLIT)]
        v_hi = [sb(f"v_hi{b}", [P, SPLIT, GH * D], F32R) for b in range(BATCH)]
        v_lo = [sb(f"v_lo{b}", [P, SPLIT, GH * D], F32R) for b in range(BATCH)]
        v_last = [sb(f"v_last{b}", [P, GH * D]) for b in range(BATCH)]
        pf = sb("pf", [P, sum(P_LEN)])
        p_hi = sb("p_hi", [P, P_COLS], F32R)
        p_lo = sb("p_lo", [P, P_COLS], F32R)
        tanh_g = sb("tanh_g", [P, SEQ])
        square = sb("square", [P, SEQ])
        gated = sb("gated", [P, SEQ])
        g_hi = [sb(f"g_hi{s}", [P, SEQ], F32R) for s in range(STEPS)]
        g_lo = [sb(f"g_lo{s}", [P, SEQ], F32R) for s in range(STEPS)]
        sum_sq = sb("sum_sq", [P, BATCH, SEQ])
        ident = sb("ident", [P, P])
        ones = sb("ones", [P, 1])
        slope = sb("slope", [P, HEADS])
        far = sb("far", [P, 2, HEADS])
        norm = sb("norm", [P, HEADS])
        half_norm = sb("half_norm", [P, HEADS])
        minus_half = sb("minus_half", [P, NTB])
        stats = sb("stats", [P, NTB, 6])
        mean_var = sb("mean_var", [P, NTB, 2])
        rs = sb("rs", [P, 4, NTB])

        diff = square[:, 0:2 * P]
        free = decay[:, :, :].rearrange("p h n -> p (h n)")
        taken = [0]

        def take(*shape):
            n = 1
            for d in shape:
                n *= d
            part = free[:, taken[0]:taken[0] + n]
            taken[0] += n
            if len(shape) == 1:
                return part
            names = "abc"[:len(shape)]
            sizes = {k: d for k, d in zip(names, shape)}
            return part.rearrange(f"p ({' '.join(names)}) -> p {' '.join(names)}", **sizes)

        x_again = take(NTB, HID)
        ar = take(KC, ER + EXPERTS)
        base_b = take(HID)
        h_keep = take(NTB, ER)
        sm = [take(NTB, EXPERTS) for _ in range(8)]
        sm1 = [take(NTB) for _ in range(8)]
        xf = [qf, kf, pf[:, 0:HID], pf[:, HID:2 * HID]]
        hw_hi = g_hi[0:2]
        hw_lo = g_lo[0:2]

        proj = [bank(f"proj{i}") for i in range(2)]
        score = [bank(f"score{i}") for i in range(3)]
        att = bank("att")
        outp = [bank(f"outp{i}") for i in range(2)]
        S = {j: score[i % 3][:, 0:P_LEN[j]] for i, j in enumerate(ORDER)}
        turn = [score[0], score[1], att, outp[0]]
        ffn = [proj[0], proj[1], score[2], outp[0], outp[1], att, score[0], score[1]]

        def sems(names):
            return [sem(n) for n in names.split()]

        x_in = [sem(f"x_in{t}") for t in range(NTB)]
        raw_in = [sem(f"raw_in{i}") for i in range(RAW_SLOTS)]
        slope_in, norm_in = sems("slope_in norm_in")
        late_in, again_in = sems("late_in again_in")
        stored = sem("stored")
        consts, diff_made, decay_made = sems("consts diff_made decay_made")
        ln = sem("ln")
        pow_ready, pow_done = sems("pow_ready pow_done")
        xn_ready, turned = sems("xn_ready turned")
        xhi_done, xlo_done, acc_zero = sems("xhi_done xlo_done acc_zero")
        whi_done, wlo_done = sems("whi_done wlo_done")
        proj_ready, proj_free = sems("proj_ready proj_free")
        qhi_done, qlo_done, khi_done, klo_done = sems("qhi_done qlo_done khi_done klo_done")
        vhi_done, vlo_done = sems("vhi_done vlo_done")
        gate_done = sem("gate_done")
        table_done = sem("table_done")
        scores_ready, masked, phi_done, plo_done = sems("scores_ready masked phi_done plo_done")
        att_ready, gated_done, ghi_done, glo_done = sems("att_ready gated_done ghi_done glo_done")
        square_done, summed = sems("square_done summed")
        out_ready, acc_done = sems("out_ready acc_done")
        xf_done, h_ready, h_read = sems("xf_done h_ready h_read")
        route, route_act, rms_ready = sems("route route_act rms_ready")
        hw_done, hw_turned, hwhi_done, hwlo_done = sems("hw_done hw_turned hwhi_done hwlo_done")
        xb_done, part_done, ffn_ready, result_done = sems("xb_done part_done ffn_ready result_done")

        def chunk(kind, i, c):
            hi, lo = {"qkg": (qkg_hi[i], qkg_lo[i]), "v": (wv_hi, wv_lo), "o": (wo_hi, wo_lo)}[kind]
            return hi[:, c, :], lo[:, c, :]

        def first_weights():
            return [chunk("qkg", 0, 0), chunk("v", 0, 0), chunk("v", 0, 1), chunk("qkg", 0, 1), chunk("qkg", 0, 2)]

        def weights():
            return [chunk("qkg", 1, 0), chunk("qkg", 1, 1), chunk("qkg", 1, 2), chunk("o", 0, 0), chunk("o", 0, 1),
                    chunk("qkg", 0, 0), chunk("v", 0, 0), chunk("qkg", 0, 1), chunk("qkg", 0, 2), chunk("v", 0, 1)]

        def slot_bank(s, k):
            return (PROJ0[s] + k) % 2

        block = ctx.enter_context(nc.Block())

        @block.sync
        def _(sp):
            def load(q, slot):
                sp.dma_start(raw[:, slot, :], w_chunks[bass.ds(q, 1)].rearrange("a p n -> (a p) n")).then_inc(raw_in[slot], 16)

            for t in range(NTB):
                sp.dma_start(acc[:, t, :], x_tok[:, t, :]).then_inc(x_in[t], 16)
                if t == TB - 1:
                    load(0, 0)
            for q in range(1, FIRST_CHUNKS):
                load(q, q)

            with sp.Fori(0, GROUPS) as g:
                for c in range(GROUP_CHUNKS):
                    sp.wait_ge(wlo_done, GROUP_CHUNKS * g + c + 1)
                    load(GROUP_CHUNKS * g + FIRST_CHUNKS + c, c % RAW_SLOTS)

            sp.wait_ge(table_done, 3 * HEADS)
            sp.dma_start(ar, a_router).then_inc(late_in, 16)
            sp.dma_start(base_b, b_base.rearrange("(a h) -> a h", a=1).to_broadcast([P, HID])).then_inc(again_in, 16)
            sp.dma_start(x_again, x_tok).then_inc(again_in, 16)
            for t in range(NTB):
                sp.wait_ge(result_done, t + 1)
                sp.dma_start(out_tok[:, t, :], acc[:, t, :]).then_inc(stored, 16)
            sp.wait_ge(stored, 16 * NTB)

        @block.gpsimd
        def _(pool):
            pool.iota(diff, pattern=[[-1, 2 * P]], base=0, channel_multiplier=1,
                      allow_small_or_imprecise_dtypes=True).then_inc(diff_made, 1)
            pool.wait_ge(diff_made, 1)
            pool.affine_select(out=diff, in_=diff, compare_op=ALU.is_ge, fill=-1e6, base=0,
                               pattern=[[1, 2 * P]], channel_multiplier=-1).then_inc(diff_made, 1)
            pool.memset(ident[:], 0.0).then_inc(consts, 1)
            pool.wait_ge(consts, 1)
            pool.affine_select(out=ident[:], in_=ident[:], compare_op=ALU.not_equal, fill=1.0, base=0,
                               pattern=[[-1, P]], channel_multiplier=1).then_inc(consts, 1)
            pool.memset(minus_half[:], -0.5).then_inc(consts, 1)
            pool.memset(ones[:], 1.0).then_inc(consts, 1)
            pool.memset(sum_sq[:], 0.0).then_inc(consts, 1)
            def power(n, cols):
                pool.wait_ge(consts, 3)
                pool.wait_ge(pow_ready, n)
                pool.tensor_tensor(rs[:, 1, cols], rs[:, 0, cols], minus_half[:, cols], ALU.pow).then_inc(pow_done, 1)

            def split_lo(hi, lo, n, slot):
                pool.wait_ge(whi_done, n + 1)
                pool.tensor_tensor(lo, raw[:, slot, :], hi.bitcast(F32), ALU.subtract).then_inc(wlo_done, 1)

            first = first_weights()
            power(1, slice(0, TB))
            pool.wait_ge(raw_in[0], 16)
            pool.tensor_copy(first[0][0], raw[:, 0, :]).then_inc(whi_done, 1)
            for n, (hi, lo) in enumerate(first):
                split_lo(hi, lo, n, n)
                if n == 2:
                    power(2, slice(TB, NTB))
            pool.wait_ge(turned, NTB)
            pool.memset(acc[:], 0.0).then_inc(acc_zero, 1)

            def add_square(n, b):
                pool.wait_ge(square_done, n + 1)
                at_least(pool, summed, n)
                pool.tensor_tensor(sum_sq[:, b, :], sum_sq[:, b, :], square[:], ALU.add).then_inc(summed, 1)

            pool.wait_ge(consts, CONSTS)

            def group(g, first=False):
                chunks = weights()
                c = 0
                for s in range(STEPS):
                    n = STEPS * g + s
                    for i in range(CHUNKS_OF_STEP[s]):
                        if i == 1 and not (first and s == 0):
                            add_square(n - 1, (s - 1) % 2)
                        hi, lo = chunks[c]
                        split_lo(hi, lo, GROUP_CHUNKS * g + FIRST_CHUNKS + c, c % RAW_SLOTS)
                        c += 1

            group(0, first=True)
            with pool.Fori(1, GROUPS) as g:
                group(g)
            add_square(STEPS * GROUPS - 1, 1)
            pool.wait_ge(again_in, 32)
            for t in range(NTB):
                pool.tensor_tensor(x_again[:, t, :], x_again[:, t, :], base_b[:], ALU.add).then_inc(xb_done, 1)
            power(3, slice(0, NTB))

        @block.scalar
        def _(act):
            act.dma_start(slope[:], slopes.rearrange("(a h) -> a h", a=1).to_broadcast([P, HEADS])).then_inc(slope_in, 16)
            act.dma_start(norm[:], norm_w).then_inc(norm_in, 16)
            act.preload_act_table_set("exp_and_others")
            act.wait_ge(diff_made, 2)

            def decays(heads):
                for h in heads:
                    act.activation(decay[:, h, :], diff, ACT.Exp, scale=SLOPES[h]).then_inc(decay_made, 1)

            def transposed_hi(b):
                for t in range(b * TB, (b + 1) * TB):
                    act.wait_ge(turned, t + 1)
                    act.activation(xhi[:, :, t * P:(t + 1) * P], turn[t % 4][:, :].rearrange("p (c n) -> p c n", c=KC),
                                   ACT.Copy).then_inc(xhi_done, 1)

            def split_hi(hi, slot):
                act.activation(hi, raw[:, slot, :], ACT.Copy).then_inc(whi_done, 1)

            decays(range(EARLY_HEADS))
            transposed_hi(0)
            act.wait_ge(whi_done, 1)

            def first_hi(chunks):
                for n in chunks:
                    act.wait_ge(raw_in[n], 16)
                    split_hi(first_weights()[n][0], n)
                if 1 in chunks:
                    decays(range(EARLY_HEADS, HEADS))
                    act.wait_ge(slope_in, 16)
                    for i in range(2):
                        act.activation(far[:, i, :], slope[:], ACT.Exp, scale=-float(P * (i + 1))).then_inc(decay_made, 1)

            first_hi((1, 2))
            act.preload_act_table_set("silu_and_others")

            def group(g, first=False):
                chunks = weights()
                c = 0
                for s in range(STEPS):
                    n = STEPS * g + s
                    h, b = s // 2, s % 2
                    slot = PROJ * g + PROJ0[s]
                    has_before = not (first and s == 0)

                    def weight():
                        nonlocal c
                        act.wait_ge(raw_in[c % RAW_SLOTS], 16 * (2 * g + 2 + c // RAW_SLOTS))
                        if c == 0:
                            at_least(act, proj_ready, PROJ * g)
                            if first:
                                act.wait_ge(wlo_done, FIRST_CHUNKS)
                        if c == 3:
                            at_least(act, out_ready, NTB * g)
                        if c == 5:
                            act.wait_ge(proj_ready, PROJ * g + PROJ0[2])
                        split_hi(chunks[c][0], c % RAW_SLOTS)
                        c += 1

                    act.wait_ge(proj_ready, slot + 1)
                    at_least(act, scores_ready, TB * n)
                    act.activation(qf[:], proj[slot_bank(s, 0)][:, :], ACT.Silu).then_inc(proj_free, 1)
                    if has_before:
                        weight()
                    else:
                        first_hi((3, 4))
                    act.wait_ge(proj_free, slot + 1)
                    act.activation(q_hi[:], qf[:], ACT.Copy).then_inc(qhi_done, 1)
                    if has_before:
                        act.wait_ge(att_ready, n)
                        at_least(act, summed, n - 1)
                        act.activation(square[:], att[:, :], ACT.Square).then_inc(square_done, 1)
                        weight()
                        act.wait_ge(gated_done, n)
                        if s == 1:
                            at_least(act, out_ready, NTB * g - TB)
                        if s == 2:
                            at_least(act, out_ready, NTB * g)
                        act.activation(g_hi[(s - 1) % STEPS][:], gated[:], ACT.Copy).then_inc(ghi_done, 1)
                    if s < BATCH:
                        at_least(act, att_ready, STEPS * g - 1 + s)
                        for t in range(TB + 1):
                            if t < TB:
                                act.wait_ge(proj_ready, slot + 2 + t)
                                if t < SPLIT:
                                    at_least(act, vlo_done, SPLIT * (BATCH * g + s - 1) + t + 1)
                                act.activation(vf[t][:] if t < SPLIT else v_last[s][:],
                                               proj[slot_bank(s, 1 + t)][:, 0:GH * D], ACT.Silu).then_inc(proj_free, 1)
                            if 1 <= t <= SPLIT:
                                act.wait_ge(proj_free, slot + 1 + t)
                                act.activation(v_hi[s][:, t - 1, :], vf[t - 1][:], ACT.Copy).then_inc(vhi_done, 1)
                    if not has_before:
                        weight()
                        weight()
                    k_slot = 1 + (TB if s < BATCH else 0)
                    act.wait_ge(proj_ready, slot + k_slot + 1)
                    act.activation(kf[:], proj[slot_bank(s, k_slot)][:, :], ACT.Silu).then_inc(proj_free, 1)
                    if CHUNKS_OF_STEP[s] == 3:
                        weight()
                    act.wait_ge(proj_free, slot + k_slot + 1)
                    act.activation(k_hi[:], kf[:, 0:SPLIT * P], ACT.Copy).then_inc(khi_done, 1)
                    if first and s == 0:
                        transposed_hi(1)
                    act.wait_ge(proj_ready, slot + k_slot + 2)
                    at_least(act, gated_done, n)
                    act.activation(tanh_g[:], proj[slot_bank(s, k_slot + 1)][:, :], ACT.Tanh,
                                   scale=0.5).then_inc(proj_free, 1)
                    for j in range(SPLIT):
                        act.wait_ge(masked, TB * n + ORDER.index(j) + 1)
                        cols = slice(P_AT[j], P_AT[j] + P_LEN[j])
                        act.activation(p_hi[:, cols], pf[:, cols], ACT.Copy).then_inc(phi_done, 1)

            group(0, first=True)
            with act.Fori(1, GROUPS) as g:
                group(g)

            N = STEPS * GROUPS
            act.wait_ge(att_ready, N)
            act.wait_ge(summed, N - 1)
            act.activation(square[:], att[:, :], ACT.Square).then_inc(square_done, 1)
            act.wait_ge(gated_done, N)
            act.activation(g_hi[STEPS - 1][:], gated[:], ACT.Copy).then_inc(ghi_done, 1)
            act.wait_ge(route, 2)
            act.activation(sm[2], sm[1], ACT.Exp).then_inc(route_act, 1)
            for t in range(2):
                act.wait_ge(hw_turned, t + 1)
                act.activation(hw_hi[t][:], score[t][:, :], ACT.Copy).then_inc(hwhi_done, 1)

        @block.vector
        def _(dve):
            done = [0]

            def link(ins):
                done[0] += 1
                ins.then_inc(ln, 1)
                dve.wait_ge(ln, done[0])

            def refine(k, cols):
                v, y, a, b = (rs[:, i, cols] for i in range(4))
                dve.wait_ge(pow_done, k)
                link(dve.tensor_tensor(a, y, y, ALU.mult))
                link(dve.tensor_tensor(b, a, v, ALU.mult))
                link(dve.tensor_scalar(a, b, -0.5, 1.5, ALU.mult, ALU.add))
                link(dve.tensor_tensor(y, y, a, ALU.mult))

            def statistics(b):
                for t in range(b * TB, (b + 1) * TB):
                    dve.wait_ge(x_in[t], 16)
                    dve.bn_stats(stats[:, t, :], acc[:, t, :]).then_inc(ln, 1)
                done[0] += TB
                dve.wait_ge(ln, done[0])
                for t in range(b * TB, (b + 1) * TB):
                    dve.bn_aggr(mean_var[:, t, :], stats[:, t, :]).then_inc(ln, 1)
                done[0] += TB
                dve.wait_ge(ln, done[0])
                cols = slice(b * TB, (b + 1) * TB)
                dve.tensor_scalar(rs[:, 0, cols], mean_var[:, cols, 1], EPS, None, ALU.add).then_inc(pow_ready, 1)

            def normalise(b):
                dve.wait_ge(pow_ready, b + 1)
                refine(b + 1, slice(b * TB, (b + 1) * TB))
                for t in range(b * TB, (b + 1) * TB):
                    dve.tensor_scalar(acc[:, t, :], acc[:, t, :], mean_var[:, t, 0:1], rs[:, 1, t:t + 1],
                                      ALU.subtract, ALU.mult).then_inc(xn_ready, 1)

            def transposed_lo(b):
                for t in range(b * TB, (b + 1) * TB):
                    dve.wait_ge(xhi_done, t + 1)
                    dve.tensor_tensor(xlo[:, :, t * P:(t + 1) * P],
                                      turn[t % 4][:, :].rearrange("p (c n) -> p c n", c=KC),
                                      xhi[:, :, t * P:(t + 1) * P].bitcast(F32), ALU.subtract).then_inc(xlo_done, 1)

            statistics(0)
            normalise(0)
            transposed_lo(0)
            statistics(1)
            normalise(1)
            dve.wait_ge(decay_made, HEADS + 2)
            dve.wait_ge(norm_in, 16)
            link(dve.tensor_scalar(half_norm[:], norm[:], 0.5, None, ALU.mult))

            def finish_att(g, s):
                n = STEPS * g + s
                dve.wait_ge(square_done, n + 1)
                dve.wait_ge(gate_done, n + 1)
                at_least(dve, glo_done, n)
                dve.tensor_tensor(gated[:], att[:, :], tanh_g[:], ALU.mult).then_inc(gated_done, 1)

            def gated_lo(g, s):
                n = STEPS * g + s
                dve.wait_ge(ghi_done, n + 1)
                dve.tensor_tensor(g_lo[s][:], gated[:], g_hi[s][:].bitcast(F32), ALU.subtract).then_inc(glo_done, 1)

            def add_out(o, b):
                for t in range(TB):
                    dve.wait_ge(out_ready, o + t + 1)
                    dve.tensor_tensor(acc[:, b * TB + t, :], acc[:, b * TB + t, :], outp[t % 2][:, :],
                                      ALU.add).then_inc(acc_done, 1)

            def group(g, first=False):
                for s in range(STEPS):
                    n = STEPS * g + s
                    h, b = s // 2, s % 2
                    if b == 0:
                        head = GH * g + h
                        at_least(dve, masked, TB * n)
                        dve.tensor_copy(table[:, 0:2 * P], decay[:, bass.ds(head, 1), :].rearrange("p a n -> p (a n)")).then_inc(table_done, 1)
                        for i in range(2):
                            dve.tensor_scalar(table[:, (2 + i) * P:(3 + i) * P],
                                              decay[:, bass.ds(head, 1), P:2 * P].rearrange("p a n -> p (a n)"),
                                              far[:, i, bass.ds(head, 1)], None, ALU.mult).then_inc(table_done, 1)
                    dve.wait_ge(qhi_done, n + 1)
                    dve.tensor_tensor(q_lo[:], qf[:], q_hi[:].bitcast(F32), ALU.subtract).then_inc(qlo_done, 1)
                    if not (first and s == 0):
                        before = (g, s - 1) if s else (g - 1, STEPS - 1)
                        finish_att(*before)
                        gated_lo(*before)
                    if s < BATCH:
                        for t in range(SPLIT):
                            dve.wait_ge(vhi_done, SPLIT * (BATCH * g + s) + t + 1)
                            dve.tensor_tensor(v_lo[s][:, t, :], vf[t][:], v_hi[s][:, t, :].bitcast(F32),
                                              ALU.subtract).then_inc(vlo_done, 1)
                    dve.wait_ge(khi_done, n + 1)
                    dve.tensor_tensor(k_lo[:], kf[:, 0:SPLIT * P], k_hi[:].bitcast(F32), ALU.subtract).then_inc(klo_done, 1)
                    if first and s == 0:
                        transposed_lo(1)
                    if first and s == 3:
                        dve.wait_ge(acc_zero, 1)
                    if s == 3:
                        add_out(NTB * g, 0)
                    if s == 0 and not first:
                        add_out(NTB * g - TB, 1)
                    if b == 0:
                        dve.wait_ge(table_done, 3 * (GH * g + h) + 3)
                    for i, j in enumerate(ORDER):
                        dve.wait_ge(scores_ready, TB * n + i + 1)
                        at_least(dve, plo_done, SPLIT * n)
                        dve.tensor_tensor(pf[:, P_AT[j]:P_AT[j] + P_LEN[j]], S[j], table[:, 0:P_LEN[j]],
                                          ALU.mult).then_inc(masked, 1)
                    for j in range(SPLIT):
                        dve.wait_ge(phi_done, SPLIT * n + j + 1)
                        cols = slice(P_AT[j], P_AT[j] + P_LEN[j])
                        dve.tensor_tensor(p_lo[:, cols], pf[:, cols], p_hi[:, cols].bitcast(F32),
                                          ALU.subtract).then_inc(plo_done, 1)
                    dve.wait_ge(proj_free, PROJ * g + PROJ0[s] + 3 + (TB if s < BATCH else 0))
                    dve.tensor_scalar(tanh_g[:], tanh_g[:], 1.0, half_norm[:, bass.ds(GH * g + h, 1)],
                                      ALU.add, ALU.mult).then_inc(gate_done, 1)

            group(0, first=True)
            with dve.Fori(1, GROUPS) as g:
                group(g)

            def make_xf(t):
                if t >= 4:
                    dve.wait_ge(h_ready, t - 3)
                dve.tensor_tensor(xf[t % 4][:, :].rearrange("p (c n) -> p c n", c=KC),
                                  xhi[:, :, t * P:(t + 1) * P].bitcast(F32),
                                  xlo[:, :, t * P:(t + 1) * P].bitcast(F32), ALU.add).then_inc(xf_done, 1)

            def read_h(t):
                dve.wait_ge(h_ready, t + 1)
                dve.tensor_copy(h_keep[:, t, :], score[t % 2][:, 0:ER]).then_inc(h_read, 1)
                dve.tensor_copy(sm[0][:, t, :], score[t % 2][:, ER:ER + EXPERTS]).then_inc(h_read, 1)

            dve.wait_ge(plo_done, SPLIT * STEPS * GROUPS)
            for t in range(3):
                make_xf(t)
            for t in range(NTB):
                read_h(t)
                if t + 3 < NTB:
                    make_xf(t + 3)
            dve.wait_ge(h_read, 2 * NTB)

            def experts(a):
                return a.unsqueeze(2).to_broadcast([P, NTB, EXPERTS])

            link(dve.tensor_reduce(sm1[0], sm[0], AX.X, ALU.max))
            dve.tensor_tensor(sm[1], sm[0], experts(sm1[0]), ALU.subtract).then_inc(route, 2)
            finish_att(GROUPS - 1, STEPS - 1)
            gated_lo(GROUPS - 1, STEPS - 1)
            dve.wait_ge(route_act, 1)
            link(dve.tensor_reduce(sm1[1], sm[2], AX.X, ALU.add))
            link(dve.reciprocal(sm1[2], sm1[1]))
            link(dve.tensor_tensor(sm[3], sm[2], experts(sm1[2]), ALU.mult))
            for e in range(EXPERTS):
                dve.memset(sm[4][:, :, e:e + 1], float(EXPERTS - e)).then_inc(ln, 1)
            done[0] += EXPERTS
            dve.wait_ge(ln, done[0])
            for k in range(TOP_K):
                left = 3 if k == 0 else 5
                if k == 0:
                    add_out(NTB * GROUPS - TB, 1)
                link(dve.tensor_reduce(sm1[3 + k], sm[left], AX.X, ALU.max))
                link(dve.tensor_tensor(sm[6], sm[left], experts(sm1[3 + k]), ALU.is_equal))
                link(dve.tensor_tensor(sm[6], sm[6], sm[4], ALU.mult))
                link(dve.tensor_reduce(sm1[5], sm[6], AX.X, ALU.max))
                link(dve.tensor_tensor(sm[6], sm[4], experts(sm1[5]), ALU.is_equal))
                if k == 0:
                    link(dve.scalar_tensor_tensor(out=sm[5], in0=sm[6], scalar=-4.0,
                                                  in1=sm[3], op0=ALU.mult, op1=ALU.add))
                    link(dve.tensor_copy(sm[7], sm[6]))
                else:
                    link(dve.tensor_tensor(sm[7], sm[7], sm[6], ALU.add))
            link(dve.tensor_tensor(sm1[5], sm1[3], sm1[4], ALU.add))
            link(dve.reciprocal(sm1[6], sm1[5]))
            link(dve.scalar_tensor_tensor(out=sm[6], in0=sm[3], scalar=LORA_SCALING,
                                          in1=sm[7], op0=ALU.mult, op1=ALU.mult))
            link(dve.tensor_tensor(sm[5], sm[6], experts(sm1[6]), ALU.mult))
            for t in range(NTB):
                hv = h_keep[:, t, :].rearrange("p (e r) -> p e r", e=EXPERTS)
                dve.tensor_tensor(hv, hv, sm[5][:, t, :].unsqueeze(2).to_broadcast([P, EXPERTS, RANK]),
                                  ALU.mult).then_inc(hw_done, 1)
            dve.wait_ge(rms_ready, 1)
            dve.tensor_scalar(rs[:, 0, :], att[:, 0:NTB], 1.0 / (HEADS * D), EPS, ALU.mult, ALU.add).then_inc(pow_ready, 1)
            for t in range(2):
                dve.wait_ge(hwhi_done, t + 1)
                dve.tensor_tensor(hw_lo[t][:], score[t][:, :], hw_hi[t][:].bitcast(F32), ALU.subtract).then_inc(hwlo_done, 1)
            dve.wait_ge(pow_ready, 3)
            refine(3, slice(0, NTB))
            dve.wait_ge(acc_done, NTB * GROUPS)

            def add_ffn(t):
                dve.wait_ge(part_done, t + 1)
                dve.wait_ge(ffn_ready, t + 1)
                dve.tensor_tensor(acc[:, t, :], ffn[t][:, :], acc[:, t, :], ALU.add).then_inc(result_done, 1)

            for t in range(NTB):
                dve.wait_ge(xb_done, t + 1)
                dve.scalar_tensor_tensor(out=acc[:, t, :], in0=acc[:, t, :], scalar=rs[:, 1, t:t + 1],
                                         in1=x_again[:, t, :], op0=ALU.mult, op1=ALU.add).then_inc(part_done, 1)
                if t >= 1:
                    add_ffn(t - 1)
            add_ffn(NTB - 1)

        @block.tensor
        def _(pe):
            def three(out_, a_hi, a_lo, b_hi, b_lo, start, stop):
                pe.matmul(out_, a_hi, b_hi, start=start, stop=False)
                pe.matmul(out_, a_hi, b_lo, start=False, stop=False)
                return pe.matmul(out_, a_lo, b_hi, start=False, stop=stop)

            def transposes(b):
                for t in range(b * TB, (b + 1) * TB):
                    pe.wait_ge(xn_ready, t + 1)
                    at_least(pe, xlo_done, t - 3)
                    for c in range(KC):
                        mm = pe.transpose(turn[t % 4][:, c * P:(c + 1) * P], acc[:, t, c * P:(c + 1) * P], ident[:])
                    mm.then_inc(turned, 1)

            def project(g, s, h, c, k):
                b = s % 2
                slot = PROJ * g + PROJ0[s] + k
                at_least(pe, proj_free, slot - 1)
                for kc in range(KC):
                    w = slice(kc * P, (kc + 1) * P)
                    x_ = slice(b * SEQ, (b + 1) * SEQ)
                    mm = three(proj[slot_bank(s, k)][:, :], qkg_hi[h][:, c, w], qkg_lo[h][:, c, w],
                               xhi[:, kc, x_], xlo[:, kc, x_], kc == 0, kc == KC - 1)
                mm.then_inc(proj_ready, 1)

            def project_v(g, s):
                for t in range(TB):
                    slot = PROJ * g + PROJ0[s] + 1 + t
                    at_least(pe, proj_free, slot - 1)
                    tok = slice((s * TB + t) * P, (s * TB + t + 1) * P)
                    for kc in range(KC):
                        w = slice((kc % 2) * 256, (kc % 2) * 256 + 256)
                        mm = three(proj[slot_bank(s, 1 + t)][:, 0:GH * D], xhi[:, kc, tok], xlo[:, kc, tok],
                                   wv_hi[:, kc // 2, w], wv_lo[:, kc // 2, w], kc == 0, kc == KC - 1)
                    mm.then_inc(proj_ready, 1)

            def attend(g, s):
                n = STEPS * g + s
                h, b = s // 2, s % 2
                pe.wait_ge(plo_done, SPLIT * (n + 1))
                at_least(pe, gated_done, n)
                e = slice(h * D, (h + 1) * D)
                for j in range(SPLIT):
                    cols = slice(P_AT[j], P_AT[j] + P_LEN[j])
                    three(att[:, j * P:SEQ], v_hi[b][:, j, e], v_lo[b][:, j, e], p_hi[:, cols], p_lo[:, cols],
                          j == 0, False)
                pe.matmul(att[:, SPLIT * P:SEQ], v_last[b][:, e], pf[:, P_AT[SPLIT]:P_AT[SPLIT] + P],
                          start=False, stop=True).then_inc(att_ready, 1)

            def output(o, b, g, last_step):
                pe.wait_ge(glo_done, STEPS * g + last_step + 1)
                pe.wait_ge(wlo_done, GROUP_CHUNKS * g + FIRST_CHUNKS + 5)
                for t in range(TB):
                    at_least(pe, acc_done, o + t - 1)
                    for h in range(GH):
                        s = h * BATCH + b
                        tok = slice(t * P, (t + 1) * P)
                        mm = three(outp[t % 2][:, :], g_hi[s][:, tok], g_lo[s][:, tok], wo_hi[:, h, :], wo_lo[:, h, :],
                                   h == 0, h == GH - 1)
                    mm.then_inc(out_ready, 1)

            def scores(g, s):
                n = STEPS * g + s
                pe.wait_ge(klo_done, n + 1)
                for i, j in enumerate(ORDER):
                    key = slice(j * P, (j + 1) * P)
                    if i == 3:
                        pe.wait_ge(masked, TB * n + 1)
                    if j == SPLIT:
                        mm = pe.matmul(S[j], kf[:, key], qf[:, key], start=True, stop=True)
                    else:
                        mm = three(S[j], k_hi[:, key], k_lo[:, key], q_hi[:, j * P:SEQ], q_lo[:, j * P:SEQ], True, True)
                    mm.then_inc(scores_ready, 1)

            def group(g, first=False):
                for s in range(STEPS):
                    h = s // 2
                    if s == 0:
                        pe.wait_ge(wlo_done, GROUP_CHUNKS * g + 1)
                    if s == 2:
                        pe.wait_ge(wlo_done, GROUP_CHUNKS * g + FIRST_CHUNKS + 3)
                    project(g, s, h, 0, 0)
                    if s:
                        attend(g, s - 1)
                    elif not first:
                        attend(g - 1, STEPS - 1)
                    k = 1
                    if s == 0:
                        pe.wait_ge(wlo_done, 3 if first else GROUP_CHUNKS * g + FIRST_CHUNKS)
                    if s < BATCH:
                        project_v(g, s)
                        k += TB
                    if first and s == 0:
                        pe.wait_ge(wlo_done, FIRST_CHUNKS)
                    project(g, s, h, 1, k)
                    if first and s == 0:
                        transposes(1)
                    project(g, s, h, 2, k + 1)
                    if s == 0 and not first:
                        output(NTB * g - TB, 1, g - 1, 3)
                    if s == 3:
                        output(NTB * g, 0, g, 2)
                    if first and s == 0:
                        pe.wait_ge(xlo_done, NTB)
                    scores(g, s)

            pe.wait_ge(consts, CONSTS)
            transposes(0)
            pe.wait_ge(xlo_done, TB)
            group(0, first=True)
            with pe.Fori(1, GROUPS) as g:
                group(g)

            def base(t):
                tok = slice(t * P, (t + 1) * P)
                for kc in range(KC):
                    w_hi, w_lo = (qkg_hi[0][:, kc, :], qkg_lo[0][:, kc, :]) if kc < 3 else (wv_hi[:, 0, :], wv_lo[:, 0, :])
                    three(ffn[t][:, :], xhi[:, kc, tok], xlo[:, kc, tok], w_hi, w_lo, kc == 0, False)

            def expert(t):
                tok = slice((t % TB) * P, (t % TB + 1) * P)
                mm = three(ffn[t][:, :], hw_hi[t // TB][:, tok], hw_lo[t // TB][:, tok], wv_hi[:, 1, :],
                           wv_lo[:, 1, :], False, True)
                mm.then_inc(ffn_ready, 1)

            pe.wait_ge(wlo_done, GROUP_CHUNKS * GROUPS + FIRST_CHUNKS)
            pe.wait_ge(proj_free, PROJ * GROUPS)
            base(0)
            base(1)
            pe.wait_ge(late_in, 16)
            for t in range(NTB):
                pe.wait_ge(xf_done, t + 1)
                if t >= 2:
                    pe.wait_ge(h_read, 2 * (t - 1))
                for kc in range(KC):
                    mm = pe.matmul(score[t % 2][:, 0:ER + EXPERTS], xf[t % 4][:, kc * P:(kc + 1) * P], ar[:, kc, :],
                                   start=kc == 0, stop=kc == KC - 1)
                mm.then_inc(h_ready, 1)
            attend(GROUPS - 1, STEPS - 1)
            base(2)
            output(NTB * GROUPS - TB, 1, GROUPS - 1, 3)
            pe.wait_ge(gated_done, STEPS * GROUPS)
            pe.wait_ge(summed, STEPS * GROUPS)
            for t in range(NTB):
                mm = pe.matmul(att[:, t:t + 1], sum_sq[:, t // TB, (t % TB) * P:(t % TB + 1) * P], ones[:],
                               start=True, stop=True)
            mm.then_inc(rms_ready, 1)
            pe.wait_ge(acc_done, NTB * GROUPS)
            base(3)
            base(4)
            for t in range(NTB):
                pe.wait_ge(hw_done, t + 1)
                mm = pe.transpose(score[t // TB][:, (t % TB) * P:(t % TB + 1) * P], h_keep[:, t, :], ident[:])
                if t % TB == TB - 1:
                    mm.then_inc(hw_turned, 1)
            pe.wait_ge(pow_ready, 3)
            base(5)
            pe.wait_ge(hwlo_done, 2)
            for t in range(NTB):
                if t >= 6:
                    base(t)
                expert(t)


def kernel(L0_attn_hidden_states, L0_attn_qkv_w, L0_attn_out_w, L0_attn_gate_w, L0_attn_norm_w,
           L0_ffn_W_base, L0_ffn_b_base, L0_ffn_W_router, L0_ffn_A, L0_ffn_B):
    import numpy as np
    import concourse.bacc as bacc
    from concourse import mybir as mb
    from concourse.bass_utils import run_bass_kernel_spmd

    def rows(w):
        return np.asarray(w).T.reshape(KC, P, -1).transpose(1, 0, 2)

    qkv = np.asarray(L0_attn_qkv_w).reshape(HEADS, 3, D, KC, P)
    gate = np.asarray(L0_attn_gate_w).reshape(HEADS, 1, D, KC, P)
    qkg = np.concatenate([qkv[:, 0:2], gate], axis=1).transpose(0, 4, 1, 3, 2).reshape(HEADS, P, 3, KC * P)
    v = qkv[:, 2].reshape(GROUPS, GH, D, KC, P).transpose(0, 4, 3, 1, 2).reshape(GROUPS, P, 2, 512)
    o = np.asarray(L0_attn_out_w).T.reshape(HEADS, D, HID)
    base = rows(L0_ffn_W_base)
    b_t = np.asarray(L0_ffn_B).transpose(0, 2, 1).reshape(ER, HID)
    chunks = [qkg[0, :, 0], v[0, :, 0], v[0, :, 1], qkg[0, :, 1], qkg[0, :, 2]]
    for g in range(GROUPS):
        h = GH * g
        chunks += [qkg[h + 1, :, 0], qkg[h + 1, :, 1], qkg[h + 1, :, 2], o[h], o[h + 1]]
        if g < GROUPS - 1:
            chunks += [qkg[h + 2, :, 0], v[g + 1, :, 0], qkg[h + 2, :, 1], qkg[h + 2, :, 2], v[g + 1, :, 1]]
        else:
            chunks += [base[:, 0], base[:, 3], base[:, 1], base[:, 2], b_t]
    a_r = np.concatenate([rows(np.asarray(L0_ffn_A).reshape(ER, HID)), rows(L0_ffn_W_router)], axis=2)
    ins = {
        "x": np.asarray(L0_attn_hidden_states), "w_chunks": np.stack(chunks),
        "norm_w": np.asarray(L0_attn_norm_w).reshape(HEADS, D).T, "a_router": a_r,
        "b_base": np.asarray(L0_ffn_b_base), "slopes": np.array(SLOPES, np.float32),
    }
    nc = bacc.Bacc("TRN2", target_bir_lowering=False, num_devices=1)
    arrays = {n: np.ascontiguousarray(a) for n, a in ins.items()}
    args = [nc.dram_tensor(n, a.shape, mb.dt.from_np(a.dtype), kind="ExternalInput").ap() for n, a in arrays.items()]
    args.append(nc.dram_tensor("out", (BATCH, SEQ, HID), F32, kind="ExternalOutput").ap())
    build(nc, *args)
    r = run_bass_kernel_spmd(nc, [arrays], core_ids=[0])
    return r.results[0]["out"]
```
